# Optimizing a Trainium2 kernel written in Bass

```python
import numpy as np
import jax
import jax.numpy as jnp

def _softmax(x, axis=-1):
    return jax.nn.softmax(x, axis=axis)

def _gelu(x):
    return jax.nn.gelu(x, approximate=True)

def _silu(x):
    return jax.nn.silu(x)

def _sigmoid(x):
    return jax.nn.sigmoid(x)

def _layernorm(x, axis=-1, eps=1e-05):
    m = jnp.mean(x, axis=axis, keepdims=True)
    v = jnp.var(x, axis=axis, keepdims=True)
    return (x - m) / jnp.sqrt(v + eps)

def _scatter_add(tgt, idx, src, axis=0):
    return tgt.at[idx].add(src)

def _segment_sum(src, seg, n):
    return jax.ops.segment_sum(src, seg, n)
kernel_name = 'mk_flamingo_gated_d1_seqx_r4_e3b45e'

def setup_inputs(seed: int=0):
    np.random.seed(seed)
    _w = jnp.asarray

    def _rec_inputs():
        import jax
        import jax.numpy as jnp
        _rk = jax.random.key(seed)
        x = -0.0005207 + 1.001 * jax.random.normal(jax.random.fold_in(_rk, 1), (8, 256, 1024), jnp.float32)
        _lenS = 256 - jax.random.randint(jax.random.fold_in(_rk, 7), (8,), 0, max(1, 256 // 4) + 1, jnp.int32)
        _lenS2 = 256 - jax.random.randint(jax.random.fold_in(_rk, 8), (8,), 0, max(1, 256 // 4) + 1, jnp.int32)
        _ctx_4096P = jax.random.normal(jax.random.fold_in(_rk, 11), (8, 16, 1024), jnp.float32)
        _ctx_4096c = jax.random.dirichlet(jax.random.fold_in(_rk, 511), 0.3 * jnp.ones((16,), jnp.float32), (8, 256))
        _ctx_4096t = jnp.einsum('bsk,bkd->bsd', _ctx_4096c, _ctx_4096P)
        _ctx_4096t = _ctx_4096t * jax.lax.rsqrt(jnp.mean(jnp.square(_ctx_4096t)) + 1e-12) * 0.953939
        ctx_4096 = -0.00010331 + 0.999899 * (_ctx_4096t + 0.3 * jax.random.normal(jax.random.fold_in(_rk, 611), (8, 256, 1024), jnp.float32))
        _g = jax.random.normal(jax.random.fold_in(_rk, 9001), (2, 1), jnp.float32)
        _g = jnp.sign(_g) * jnp.maximum(jnp.abs(_g), 1.0) + (_g == 0) * 1.0
        g_xattn = _g[0]
        g_ffn = _g[1]
        return (x, ctx_4096, g_xattn, g_ffn)
    x, ctx_4096, g_xattn, g_ffn = _rec_inputs()

    def _L0_xattn_setup():
        import jax, jax.numpy as jnp
        import numpy as np
        B, Q, D = (8, 64, 1024)
        CTX = 1024
        H, KV, HD = (16, 4, 96)
        G = H // KV
        key = jax.random.key(seed)
        ks = jax.random.split(key, 6)
        s = 0.02
        return {'latents': jax.random.normal(ks[0], (B, Q, D), jnp.float32), 'context': jax.random.normal(ks[1], (B, CTX, D), jnp.float32), 'Wq': jax.random.normal(ks[2], (H * HD, D), jnp.float32) * s, 'Wk': jax.random.normal(ks[3], (KV * HD, D), jnp.float32) * s, 'Wv': jax.random.normal(ks[4], (KV * HD, D), jnp.float32) * s, 'Wo': jax.random.normal(ks[5], (D, H * HD), jnp.float32) * s}
    _L0_xattn_all = _L0_xattn_setup()
    _L0_xattn_in = {k: v for k, v in _L0_xattn_all.items() if k in ('Wq', 'Wk', 'Wv', 'Wo')}
    del _L0_xattn_all

    def _L0_ffn_setup():
        import jax, jax.numpy as jnp
        import numpy as np
        HID, INT, LAT, NE, K = (1024, 2048, 512, 8, 2)
        LN_EPS = 1e-05

        def _layernorm(x, gamma, beta):
            mu = jnp.mean(x, axis=-1, keepdims=True)
            var = jnp.var(x, axis=-1, keepdims=True)
            return (x - mu) * jax.lax.rsqrt(var + LN_EPS) * gamma + beta
        key = jax.random.key(seed)
        ks = jax.random.split(key, 8)
        s = lambda d: 1.0 / np.sqrt(d)
        return {'hidden_states': jax.random.normal(ks[0], (4, 512, HID), jnp.float32), 'gate_w': jax.random.normal(ks[1], (HID, NE), jnp.float32) * s(HID), 'up_w': jax.random.normal(ks[2], (HID, INT), jnp.float32) * s(HID), 'down_w': jax.random.normal(ks[3], (INT, HID), jnp.float32) * s(INT), 'fc1_w': jax.random.normal(ks[4], (HID, LAT), jnp.float32) * s(HID), 'fc2_w': jax.random.normal(ks[5], (LAT, HID), jnp.float32) * s(LAT), 'expert_w': jax.random.normal(ks[6], (LAT, LAT), jnp.float32), 'ln_gamma': jnp.ones((HID,), jnp.float32), 'ln_beta': jnp.zeros((HID,), jnp.float32)}
    _L0_ffn_all = _L0_ffn_setup()
    _L0_ffn_in = {k: v for k, v in _L0_ffn_all.items() if k in ('gate_w', 'up_w', 'down_w', 'fc1_w', 'fc2_w', 'expert_w', 'ln_gamma', 'ln_beta')}
    del _L0_ffn_all
    return {'x': x, 'ctx_4096': ctx_4096, 'g_xattn': g_xattn, 'g_ffn': g_ffn, 'L0_xattn_Wq': _L0_xattn_in['Wq'], 'L0_xattn_Wk': _L0_xattn_in['Wk'], 'L0_xattn_Wv': _L0_xattn_in['Wv'], 'L0_xattn_Wo': _L0_xattn_in['Wo'], 'L0_ffn_gate_w': _L0_ffn_in['gate_w'], 'L0_ffn_up_w': _L0_ffn_in['up_w'], 'L0_ffn_down_w': _L0_ffn_in['down_w'], 'L0_ffn_fc1_w': _L0_ffn_in['fc1_w'], 'L0_ffn_fc2_w': _L0_ffn_in['fc2_w'], 'L0_ffn_expert_w': _L0_ffn_in['expert_w'], 'L0_ffn_ln_gamma': _L0_ffn_in['ln_gamma'], 'L0_ffn_ln_beta': _L0_ffn_in['ln_beta']}

def reference(x, ctx_4096, g_xattn, g_ffn, L0_xattn_Wq, L0_xattn_Wk, L0_xattn_Wv, L0_xattn_Wo, L0_ffn_gate_w, L0_ffn_up_w, L0_ffn_down_w, L0_ffn_fc1_w, L0_ffn_fc2_w, L0_ffn_expert_w, L0_ffn_ln_gamma, L0_ffn_ln_beta):
    import jax
    import jax.numpy as jnp

    def _L0_xattn_ref(latents, context, Wq, Wk, Wv, Wo):
        import jax, jax.numpy as jnp
        import numpy as np
        B, Q, D = (8, 64, 1024)
        CTX = 1024
        H, KV, HD = (16, 4, 96)
        G = H // KV
        b, q_len, _ = latents.shape
        hidden = jnp.concatenate([context, latents], axis=1)
        s_len = hidden.shape[1]
        q = (latents @ Wq.T).reshape(b, q_len, H, HD)
        k = (hidden @ Wk.T).reshape(b, s_len, KV, HD)
        v = (hidden @ Wv.T).reshape(b, s_len, KV, HD)
        q = q.transpose(0, 2, 1, 3).reshape(b, KV, G, q_len, HD)
        k = k.transpose(0, 2, 1, 3)
        v = v.transpose(0, 2, 1, 3)
        scale = 1.0 / jnp.sqrt(jnp.asarray(HD, q.dtype))
        scores = jnp.einsum('bkgqd,bksd->bkgqs', q, k) * scale
        attn = jax.nn.softmax(scores.astype(jnp.float32), axis=-1).astype(q.dtype)
        out = jnp.einsum('bkgqs,bksd->bkgqd', attn, v)
        out = out.reshape(b, H, q_len, HD).transpose(0, 2, 1, 3).reshape(b, q_len, H * HD)
        return out @ Wo.T

    def _L0_ffn_ref(hidden_states, gate_w, up_w, down_w, fc1_w, fc2_w, expert_w, ln_gamma, ln_beta):
        import jax, jax.numpy as jnp
        import numpy as np
        HID, INT, LAT, NE, K = (1024, 2048, 512, 8, 2)
        LN_EPS = 1e-05

        def _layernorm(x, gamma, beta):
            mu = jnp.mean(x, axis=-1, keepdims=True)
            var = jnp.var(x, axis=-1, keepdims=True)
            return (x - mu) * jax.lax.rsqrt(var + LN_EPS) * gamma + beta
        logits = jnp.einsum('bsh,he->bse', hidden_states, gate_w)
        routing_weights, selected_experts = jax.lax.top_k(logits, K)
        h = jax.nn.relu(jnp.einsum('bsh,hi->bsi', hidden_states, up_w)) ** 2
        shared_out = jnp.einsum('bsi,ih->bsh', h, down_w)
        x_latent = jnp.einsum('bsh,hl->bsl', hidden_states, fc1_w)
        expert_out = jnp.einsum('bsl,lm->bsm', x_latent, expert_w)
        moe_out = expert_out * jnp.sum(routing_weights, axis=-1, keepdims=True)
        routed_out = jnp.einsum('bsl,lh->bsh', moe_out, fc2_w)
        return _layernorm(shared_out + routed_out, ln_gamma, ln_beta)
    x = x + jnp.tanh(g_xattn[0]) * _L0_xattn_ref(_layernorm(x, axis=-1), ctx_4096, L0_xattn_Wq, L0_xattn_Wk, L0_xattn_Wv, L0_xattn_Wo)
    x = x + jnp.tanh(g_ffn[0]) * _L0_ffn_ref(_layernorm(x, axis=-1), L0_ffn_gate_w, L0_ffn_up_w, L0_ffn_down_w, L0_ffn_fc1_w, L0_ffn_fc2_w, L0_ffn_expert_w, L0_ffn_ln_gamma, L0_ffn_ln_beta)
    return x

_drawn_inputs = setup_inputs


def setup_inputs(seed=0):
    import zlib

    import numpy as np

    out = dict(_drawn_inputs(seed))
    spreads = {'L0_ffn_ln_gamma': (1.0, 0.2), 'L0_ffn_ln_beta': (0.0, 0.1)}
    factors = {'L0_xattn_Wq': 2.762, 'L0_xattn_Wk': 2.723}
    for name, (base, spread) in spreads.items():
        noise = np.random.default_rng([zlib.crc32(name.encode()), seed]).standard_normal(out[name].shape)
        drawn = base * np.exp(spread * noise) if base else spread * noise
        out[name] = jnp.asarray(drawn.astype(out[name].dtype))
    for name, factor in factors.items():
        out[name] = (out[name] * factor).astype(out[name].dtype)
    return out
```

```python
from contextlib import ExitStack

import concourse.bass as bass
from concourse import mybir
from concourse.alu_op_type import AluOpType as ALU

F32 = mybir.dt.float32
F32R = mybir.dt.float32r
ACT = mybir.ActivationFunctionType
AX = mybir.AxisListType

BATCH, SEQ, DIM = 8, 256, 1024
KV, GROUP, HD = 4, 4, 96
INT, LAT, EXPERTS = 2048, 512, 8
EPS = 1e-5
SCALE = float(HD) ** -0.5
P = 128
TOK = 512
BLOCKS = BATCH * SEQ // TOK
BPB = TOK // SEQ
TT = TOK // P
KC = DIM // P
HT = 3
OT = KV * HT
UT = INT // P
LT = LAT // P
HALF = DIM // 2
KVW = HT * P + KV * HD
GPAD = 66
DC = (LT + UT) // 2
MXW = TT * GROUP + P - GROUP

U_CTX = 0
U_X = U_CTX + KC
U_Q = U_X + KC
U_O = U_Q + KV * HT
U_FC1 = U_O + 2 * (OT // 2)
U_UP0 = U_FC1 + LT
U_EXP = U_UP0 + 2
U_UP2 = U_EXP + LT // 2
U_DOWN = U_UP2 + UT - 2
UNITS = U_DOWN + 2 * DC
assert UNITS % 2 == 0
UNIT_UP = [U_UP0, U_UP0 + 1] + [U_UP2 + j for j in range(UT - 2)]

PRING = 6
NBANK = 8


def steps_main():
    s = [("kv", 0, kc) for kc in range(KC)] + [("kv", 1, kc) for kc in range(KC)]
    s += [("q", 0, t) for t in range(HT)] + [("max", 0, tt) for tt in range(TT)] + [("maxT", 0)]
    for g in range(KV):
        n = g + 1
        order = [("score", g, 0), ("q", n, 0), ("score", g, 1), ("q", n, 1), ("pv", g, 0), ("q", n, 2),
                 ("score", g, 2), ("max", n, 0), ("pv", g, 1), ("max", n, 1), ("max", n, 2), ("score", g, 3),
                 ("max", n, 3), ("pv", g, 2), ("maxT", n), ("pv", g, 3)]
        s += [x for x in order if x[1] == g or n < KV]
    s += [("o", h, c) for h in range(2) for c in range(OT // 2)]
    s += [("ln2T", kc) for kc in range(KC)]
    s += [("gate",), ("fc1", 0), ("gateT",), ("fc1", 1), ("fc1", 2), ("rbc",), ("fc1", 3), ("up", 0), ("up", 1)]
    s += [("exp", j) for j in range(LT)] + [("up", j) for j in range(2, UT)]
    for c in range(DC):
        s += [("down", 0, c)]
        if 1 <= c <= KC:
            s += [("ln1T", c - 1)]
    s += [("down", 1, c) for c in range(DC)]
    return s


STEPS = steps_main()


def bank_plan():
    jobs = []
    for s in STEPS:
        if s[0] == "kv" and s[2] == 0:
            jobs += [("kv", s[1], t) for t in range(HT + TT)]
        elif s[0] == "max":
            jobs += [("max", s[1], s[2], h) for h in range(GROUP)]
        elif s[0] == "score":
            jobs += [("score", s[1], s[2], kt) for kt in range(4)]
        elif s[0] == "o" and s[2] == 0:
            jobs += [("o", s[1], tt) for tt in range(TT)]
        elif s[0] in ("q", "maxT", "pv", "ln2T", "gate", "gateT", "rbc", "fc1", "exp", "up", "ln1T"):
            jobs += [s]
        elif s[0] == "down" and s[2] == 0:
            jobs += [("down", s[1], tt) for tt in range(TT)]
    plan, fills, n = {}, [0] * NBANK, 0
    for j in jobs:
        if j[0] == "down":
            b = 4 * j[1] + j[2]
        elif j[0] == "ln1T":
            b = 4 + j[1] % 4
        else:
            b, n = n % NBANK, n + 1
        fills[b] += 1
        plan[j] = (b, fills[b])
    return plan, fills


def t32_order(s):
    return s[1] if s[0] == "up" and s[1] < 2 else 2 + s[1] if s[0] == "exp" else LT + s[1]


BANK, FILLS = bank_plan()
MEAN_LINKS = 4
AHEAD_LINKS = 3 + MEAN_LINKS
DVE_LINKS = 2 * KV * 4 + 3 * (1 + MEAN_LINKS) + 1 + 3
FILLS_AHEAD = [2 if b >= 4 else 0 for b in range(NBANK)]


def fill(block, job):
    b, k = BANK[job]
    if isinstance(block, str):
        return b, 1 + job[1] // 4
    if isinstance(block, int) and block == BLOCKS - 1 and job[:2] == ("down", 1):
        k -= KC // 4
    return b, block * FILLS[b] + (FILLS_AHEAD[b] + k)


def unit_of(s):
    if s[0] == "kv":
        return (U_CTX, U_X)[s[1]] + s[2]
    if s[0] == "q":
        return U_Q + s[1] * HT + s[2]
    if s[0] == "o":
        return U_O + s[1] * (OT // 2) + s[2]
    if s[0] == "fc1":
        return U_FC1 + s[1]
    if s[0] == "exp" and s[1] % 2 == 0:
        return U_EXP + s[1] // 2
    if s[0] == "up":
        return UNIT_UP[s[1]]
    if s[0] == "down":
        return U_DOWN + s[1] * DC + s[2]
    return None


def unit_ends():
    ends = {}
    for s in STEPS:
        u = unit_of(s)
        if s[0] in ("q", "fc1", "up"):
            ends[u] = s
        elif s[0] == "exp" and s[1] % 2:
            ends[U_EXP + s[1] // 2] = s
        elif s[0] == "kv" and s[2] == KC - 1:
            ends[u] = ("kv", s[1], HT + TT - 1)
        elif s[0] == "o" and s[2] == OT // 2 - 1:
            ends[u] = ("o", s[1], TT - 1)
        elif s[0] == "down" and s[2] == DC - 1:
            ends[u] = ("down", s[1], TT - 1)
    return ends


ENDS = unit_ends()
COUNTED = [u for u in range(UNITS) if u not in ENDS]


class Count:

    def __init__(self, sem, per, credit=0, step=1):
        self.sem, self.per, self.credit, self.step = sem, per, credit, step

    def at(self, block, k):
        return block * (self.per * self.step) + (self.credit + k * self.step)


def layer_kernel(nc, x, ctxT, g_x, g_f, w_kv, w_q, w_o, w_fc1, w_exp, w_up, w_down, w_gate, gamma, beta, out):
    ctx = ExitStack()
    with ctx:
        sem = lambda name: ctx.enter_context(nc.semaphore(name))

        base = (nc.sbuf_base + 31) // 32 * 32
        top = [base]

        def region(size):
            at = top[0]
            top[0] += (size + 31) // 32 * 32
            return at

        def place(name, shape, dtype, at):
            return nc.alloc_sbuf_tensor_at(name, shape, dtype, offset=at)

        K4 = 4096
        r_x = region(8 * K4)
        r_kv = region(15 * K4)
        r_p = region(6 * K4)
        r_t32 = region(K4)
        r_o32 = region(6 * K4)
        r_qa = region(4 * K4)
        r_qb = region(4 * K4)
        r_ws = region(2 * K4)
        r_wh = region(2 * K4)
        r_wl = region(2 * K4)

        x_hi = place("x_hi", [P, KC, TOK], F32R, r_x)
        x_lo = place("x_lo", [P, KC, TOK], F32R, r_x + 4 * K4)
        k_hi = place("k_hi", [P, KV, BPB, 2, SEQ], F32R, r_kv)
        k_lo = place("k_lo", [P, KV, BPB, 2, SEQ], F32R, r_kv + 4 * K4)
        v_hi = place("v_hi", [P, 2, TT, KV, P], F32R, r_kv + 8 * K4)
        v_lo = place("v_lo", [P, 2, TT, KV, HD], F32R, r_kv + 12 * K4)
        o_hi = place("o_hi", [P, OT, TOK], F32R, r_kv)
        o_lo = place("o_lo", [P, OT, TOK], F32R, r_kv + 6 * K4)
        h_hi = place("h_hi", [P, UT, TOK], F32R, r_kv)
        h_lo = place("h_lo", [P, UT, TOK], F32R, r_kv + 8 * K4)
        p_hi = place("p_hi", [P, PRING, 2, SEQ], F32R, r_p)
        p_lo = place("p_lo", [P, PRING, 2, SEQ], F32R, r_p + 3 * K4)
        x2 = place("x2", [P, TT, DIM], F32, r_p + K4)
        t32 = place("t32", [P, 2, TOK], F32, r_t32)
        o32 = place("o32", [P, OT, TOK], F32, r_o32)
        rows = place("rows", [P, TT, DIM], F32, r_o32)
        gate_log = place("gate_log", [P, TOK], F32, r_o32)
        r_diag = place("r_diag", [P, TOK], F32, r_o32 + K4)
        r_bc = place("r_bc", [P, TOK], F32, r_o32 + 2 * K4)
        gate_ones = place("gate_ones", [P, P], F32, r_o32 + 3 * K4)
        gam = place("gam", [P, DIM], F32, r_o32 + 4 * K4)
        bet = place("bet", [P, DIM], F32, r_o32 + 5 * K4)
        qa_hi = place("qa_hi", [P, GROUP, TOK], F32R, r_qa)
        qa_lo = place("qa_lo", [P, GROUP, TOK], F32R, r_qa + 2 * K4)
        lat_hi = place("lat_hi", [P, LT, TOK], F32R, r_qa)
        lat_lo = place("lat_lo", [P, LT, TOK], F32R, r_qa + 2 * K4)
        y = place("y", [P, TT, DIM], F32, r_qa)
        qb_hi = place("qb_hi", [P, GROUP, TOK], F32R, r_qb)
        qb_lo = place("qb_lo", [P, GROUP, TOK], F32R, r_qb + 2 * K4)
        c_st = place("c_st", [P, 2, TOK], F32, r_qb)
        c_hi = place("c_hi", [P, 2, TOK], F32R, r_qb + K4)
        c_lo = place("c_lo", [P, 2, TOK], F32R, r_qb + 2 * K4)
        moe_hi = place("moe_hi", [P, LT, TOK], F32R, r_qb)
        moe_lo = place("moe_lo", [P, LT, TOK], F32R, r_qb + 2 * K4)
        w_st = place("w_st", [P, 2, DIM], F32, r_ws)
        w_hi = place("w_hi", [P, 2, DIM], F32R, r_wh)
        w_lo = place("w_lo", [P, 2, DIM], F32R, r_wl)
        ident = place("ident", [P, P], F32, region(4 * P))
        gate_w = place("gate_w", [P, KC, GPAD], F32R, region(4 * KC * GPAD))
        inv_guess = place("inv_guess", [32, BPB, SEQ], F32, region(4 * TOK))
        neg_inv = place("neg_inv", [32, BPB, SEQ], F32, region(4 * TOK))
        gate_st = place("gate_st", [P, KC, EXPERTS], F32, r_t32)
        row_max = place("row_max", [P, MXW], F32, region(4 * MXW))
        neg_mask = place("neg_mask", [GROUP, GROUP], F32, region(32))
        bn = place("bn", [P, TT, 2, 6], F32, region(192))
        mv = place("mv", [P, TT, 2], F32, region(32))
        var = place("var", [P, TT], F32, region(32))
        rstd0 = place("rstd0", [P, TT], F32, region(32))
        newt = place("newt", [P, TT], F32, region(32))
        rstd = place("rstd", [P, TT], F32, region(32))
        logits = place("logits", [P, TT, EXPERTS], F32, region(128))
        top8 = place("top8", [P, TT, EXPERTS], F32, region(128))
        r_sum = place("r_sum", [P, TT], F32, region(32))
        tg = place("tg", [P, 2], F32, region(32))
        assert top[0] <= nc.sbuf_usable_end, top[0] - nc.sbuf_usable_end
        q_hi, q_lo = [qb_hi, qa_hi], [qb_lo, qa_lo]

        bank = [ctx.enter_context(nc.psum_tensor(f"bank{b}", [P, TOK], F32)) for b in range(NBANK)]

        full = [sem(f"bank_full{b}") for b in range(NBANK)]
        read = [sem(f"bank_read{b}") for b in range(NBANK)]
        w_loaded = [Count(sem(f"w_loaded{s}"), UNITS // 2, step=16) for s in range(2)]
        w_hi_done = Count(sem("w_hi_done"), UNITS)
        w_ready = Count(sem("w_ready"), UNITS)
        w_used = Count(sem("w_used"), len(COUNTED))
        c_loaded = [Count(sem(f"c_loaded{s}"), KC // 2, step=16) for s in range(2)]
        c_hi_done = Count(sem("c_hi_done"), KC)
        c_ready = Count(sem("c_ready"), KC)
        x_loaded = [Count(sem(f"x_loaded{t}"), 1, step=16) for t in range(TT)]
        xn_ready = Count(sem("xn_ready"), TT)
        xn2_ready = Count(sem("xn2_ready"), TT)
        x1_hi = Count(sem("x1_hi"), KC)
        x2_hi = Count(sem("x2_hi"), KC)
        kv_hi = Count(sem("kv_hi"), 2 * (HT + TT))
        ones_ready = Count(sem("ones_ready"), 2)
        q_hi_done = Count(sem("q_hi_done"), KV * HT)
        p_used = Count(sem("p_used"), KV * 4 * 3)
        lo_ready = Count(sem("lo_ready"), KV * 16 + LT + UT)
        ln_done = Count(sem("ln_done"), KV * 4)
        inv_ready = Count(sem("inv_ready"), KV * 4)
        o_hi_done = Count(sem("o_hi_done"), OT)
        o_ready = Count(sem("o_ready"), OT)
        xres_loaded = Count(sem("xres_loaded"), 1, step=16)
        diag_ready = Count(sem("diag_ready"), 1)
        lat_hi_done = Count(sem("lat_hi_done"), LT)
        relu_done = Count(sem("relu_done"), UT)
        t_hi_done = Count(sem("t_hi_done"), LT + UT)
        gb_loaded = Count(sem("gb_loaded"), 2, step=16)
        gb_ready = Count(sem("gb_ready"), 1)
        var_ready = Count(sem("var_ready"), 3, credit=1)
        rstd_guess = Count(sem("rstd_guess"), 3, credit=1)
        lnvar_done = Count(sem("lnvar_done"), 3, credit=1)
        y_ready = Count(sem("y_ready"), TT)
        out_stored = Count(sem("out_stored"), TT, credit=1, step=16)
        small_loaded, tanh_ready, gate_hi_done = sem("small_loaded"), sem("tanh_ready"), sem("gate_hi_done")
        zeroed, ident_ready = sem("zeroed"), sem("ident_ready")
        gate_ready = sem("gate_ready")
        dve_chain = Count(sem("dve_chain"), DVE_LINKS)
        waits_ended = sem("waits_ended")
        pool_chain = Count(sem("pool_chain"), 1)

        x_rows = x.rearrange("(i t p) d -> i t p d", t=TT, p=P)
        out_rows = out.rearrange("(i t p) d -> i t p d", t=TT, p=P)
        block = ctx.enter_context(nc.Block())

        def waited(eng):
            eng.sem_inc(waits_ended, 1)

        def over_blocks(eng, body):
            with eng.Fori(0, BLOCKS - 1) as i:
                body(i, False)
            body(BLOCKS - 1, True)

        def unit_dram(u):
            if u < U_Q:
                return w_kv[u % KC], KVW
            if u < U_O:
                return w_q[u - U_Q], DIM
            if u < U_FC1:
                return w_o[u - U_O], DIM
            if u < U_UP0:
                return w_fc1[u - U_FC1], DIM
            if U_EXP <= u < U_UP2:
                return w_exp[u - U_EXP], DIM
            if u < U_DOWN:
                return w_up[UNIT_UP.index(u)], DIM
            return w_down[u - U_DOWN], DIM

        def unit_used(eng, i, u):
            if u == -1:
                b, _ = BANK[ENDS[UNITS - 1]]
                eng.wait_ge(full[b], i * FILLS[b] + FILLS_AHEAD[b])
            elif u in ENDS:
                b, v = fill(i, ENDS[u])
                eng.wait_ge(full[b], v)
            else:
                eng.wait_ge(w_used.sem, w_used.at(i, COUNTED.index(u) + 1))

        @block.sync
        def _(sp):
            def load_unit(i, u, ahead=None):
                i, u = (i, u) if u < UNITS else (i + 1, u - UNITS)
                src, n = unit_dram(u)
                if ahead is None:
                    sp.wait_ge(w_ready.sem, w_ready.at(i, u + 1 - 2))
                sp.dma_start(w_st[:, u % 2, 0:n], src).then_inc(w_loaded[u % 2].sem, 16)

            def load_ctx(i, kc):
                i, kc = (i, kc) if kc < KC else (i + 1, kc - KC)
                if kc >= 2:
                    sp.wait_ge(c_ready.sem, c_ready.at(i, kc + 1 - 2))
                    waited(sp)
                sp.dma_start(c_st[:, kc % 2, :], ctxT[i, kc]).then_inc(c_loaded[kc % 2].sem, 16)

            def load_rows(i):
                for tt in range(TT):
                    sp.dma_start(rows[:, tt, :], x_rows[i, tt]).then_inc(x_loaded[tt].sem, 16)

            load_rows(0)
            sp.dma_start(tg[:, 0:1], g_x.partition_broadcast(P)).then_inc(small_loaded, 16)
            sp.dma_start(tg[:, 1:2], g_f.partition_broadcast(P)).then_inc(small_loaded, 16)
            sp.dma_start(gate_st[:, :, :], w_gate).then_inc(small_loaded, 16)
            load_ctx(0, 0)
            load_unit(0, 0, ahead=True)
            load_ctx(0, 1)
            load_unit(0, 1, ahead=True)

            def body(i, last):
                for u in range(2, UNITS if last else UNITS + 2):
                    if u == UNITS:
                        unit_used(sp, i, UNITS - 4)
                        waited(sp)
                        load_ctx(i, KC)
                        load_ctx(i, KC + 1)
                    load_unit(i, u)
                    if u < KC:
                        load_ctx(i, u)
                    if u == U_O + 2:
                        b, v = fill(i, ("pv", KV - 1, 3))
                        sp.wait_ge(full[b], v)
                        waited(sp)
                        sp.dma_start(x2[:, :, :], x_rows[i].rearrange("t p d -> p t d")).then_inc(xres_loaded.sem, 16)
                    if u == U_FC1 - 2:
                        sp.wait_ge(o_ready.sem, o_ready.at(i, OT))
                        sp.dma_start(gam[:, :], gamma.partition_broadcast(P)).then_inc(gb_loaded.sem, 16)
                        sp.dma_start(bet[:, :], beta.partition_broadcast(P)).then_inc(gb_loaded.sem, 16)
                    if u == U_DOWN - 4 and not last:
                        b, v = fill(i, ("exp", LT - 1))
                        sp.wait_ge(read[b], v + 1)
                        waited(sp)
                        load_rows(i + 1)
                for tt in range(TT):
                    sp.wait_ge(y_ready.sem, y_ready.at(i, tt + 1))
                    waited(sp)
                    sp.dma_start(out_rows[i, tt], y[:, tt, :]).then_inc(out_stored.sem, 16)
                if last:
                    sp.wait_ge(out_stored.sem, out_stored.at(i, TT))

            over_blocks(sp, body)

        @block.scalar
        def _(act):
            copy = lambda o, i_: nc.scalar.activation(o, i_, ACT.Copy)

            def split_w(i, u, ahead=None):
                n = unit_dram(u % UNITS)[1]
                if ahead is None:
                    unit_used(act, i, u - 2)
                i, u = (i, u) if u < UNITS else (i + 1, u - UNITS)
                act.wait_ge(w_loaded[u % 2].sem, w_loaded[u % 2].at(i, u // 2 + 1))
                copy(w_hi[:, u % 2, 0:n], w_st[:, u % 2, 0:n]).then_inc(w_hi_done.sem, 1)

            def split_c(i, kc):
                i, kc = (i, kc) if kc < KC else (i + 1, kc - KC)
                act.wait_ge(c_loaded[kc % 2].sem, c_loaded[kc % 2].at(i, kc // 2 + 1))
                if kc >= 2:
                    unit_used(act, i, U_CTX + kc - 2)
                copy(c_hi[:, kc % 2, :], c_st[:, kc % 2, :]).then_inc(c_hi_done.sem, 1)

            def when_full(i, job):
                b, v = fill(i, job)
                act.wait_ge(full[b], v)
                return b

            def prob_used(i, k):
                if k % 4 == 3:
                    when_full(i, ("pv", k // 16, k // 4 % 4))
                else:
                    act.wait_ge(p_used.sem, p_used.at(i, k // 4 * 3 + k % 4 + 1))

            def guess_rstd(i, k):
                act.wait_ge(var_ready.sem, var_ready.at(i, k))
                nc.scalar.activation(rstd0[:, :], var[:, :], ACT.Ln).then_inc(lnvar_done.sem, 1)
                act.wait_ge(lnvar_done.sem, lnvar_done.at(i, k))
                nc.scalar.activation(rstd0[:, :], rstd0[:, :], ACT.Exp, scale=-0.5).then_inc(rstd_guess.sem, 1)

            act.wait_ge(small_loaded, 48)
            nc.scalar.activation(tg[:, :], tg[:, :], ACT.Tanh).then_inc(tanh_ready, 1)
            act.wait_ge(zeroed, 2)
            copy(gate_w[:, :, 0:EXPERTS], gate_st[:, :, :]).then_inc(gate_hi_done, 1)
            guess_rstd(0, 0)
            split_c(0, 0)
            split_w(0, 0, ahead=True)
            for kc in range(KC):
                b = when_full("ahead", ("ln1T", kc))
                copy(x_hi[:, kc, :], bank[b][:, :]).then_inc(x1_hi.sem, 1)

            def body(i, last):
                for s in STEPS:
                    kind, u = s[0], unit_of(s)
                    if kind == "kv" and s[1] == 0 and s[2] + 1 < KC:
                        split_c(i, s[2] + 1)
                    if kind == "o" and s[1:] == (0, 0):
                        b = when_full(i, ("pv", KV - 1, 3))
                        b, v = fill(i, ("pv", KV - 1, 3))
                        act.wait_ge(read[b], v + 1)
                        for t in range(2):
                            copy(o_hi[:, t, :], o32[:, t, :]).then_inc(o_hi_done.sem, 1)
                    if u is not None and (u + 1 < UNITS or not last):
                        split_w(i, u + 1)
                    if kind == "o" and s[1] == 0:
                        for t in range(2 * s[2] + 2, min(2 * s[2] + 4, OT)):
                            copy(o_hi[:, t, :], o32[:, t, :]).then_inc(o_hi_done.sem, 1)
                    if u == UNITS - 1 and not last:
                        split_c(i, KC)
                    if kind == "down" and s[1:] == (0, 0) and not last:
                        guess_rstd(i, 2)

                    if kind == "kv" and s[2] == KC - 1:
                        src = s[1]
                        for t in range(HT):
                            b = when_full(i, ("kv", src, t))
                            copy(k_hi[0:96, t, :, src, :], bank[b][0:96, :].rearrange("p (b s) -> p b s", b=BPB))
                            copy(k_hi[32 * t:32 * t + 32, 3, :, src, :],
                                 bank[b][96:128, :].rearrange("p (b s) -> p b s", b=BPB)).then_inc(kv_hi.sem, 1)
                        for tt in range(TT):
                            b = when_full(i, ("kv", src, HT + tt))
                            copy(v_hi[:, src, tt, :, 0:HD],
                                 bank[b][:, 0:KV * HD].rearrange("p (g d) -> p g d", g=KV)).then_inc(kv_hi.sem, 1)
                    elif kind == "q":
                        g, t = s[1:]
                        if (g, t) == (1, 0):
                            act.wait_ge(out_stored.sem, out_stored.at(i, 0))
                        b = when_full(i, s)
                        copy(q_hi[g % 2][0:96, t, :], bank[b][0:96, :])
                        copy(q_hi[g % 2][32 * t:32 * t + 32, 3, :], bank[b][96:128, :]).then_inc(q_hi_done.sem, 1)
                    elif kind == "score":
                        g, n = s[1:]
                        if (g, n) == (0, 0):
                            act.wait_ge(out_stored.sem, out_stored.at(i, 0))
                        for kt in range(4):
                            k = g * 16 + n * 4 + kt
                            b = when_full(i, s + (kt,))
                            if k >= 2:
                                act.wait_ge(lo_ready.sem, lo_ready.at(i, k + 1 - 2))
                            nc.scalar.activation(t32[:, k % 2, :], bank[b][:, :], ACT.Exp, scale=SCALE)
                            if k >= PRING:
                                prob_used(i, k - PRING)
                            nc.scalar.activation(p_hi[:, k % PRING].rearrange("p b s -> p (b s)"), bank[b][:, :],
                                                 ACT.Exp, scale=SCALE).then_inc(read[b], 1)
                    elif kind == "pv":
                        n = s[1] * 4 + s[2]
                        if n:
                            b, v = fill(i, ("pv", (n - 1) // 4, (n - 1) % 4))
                            act.wait_ge(read[b], v + 1)
                        b = when_full(i, s)
                        nc.scalar.activation(inv_guess[:, :, :], bank[b][96:128, :].rearrange("p (b s) -> p b s", b=BPB),
                                             ACT.Ln).then_inc(ln_done.sem, 1)
                        act.wait_ge(ln_done.sem, ln_done.at(i, n + 1))
                        nc.scalar.activation(inv_guess[:, :, :], inv_guess[:, :, :], ACT.Exp,
                                             scale=-1.0).then_inc(inv_ready.sem, 1)
                    elif kind == "o" and s[1:] == (1, OT // 2 - 1):
                        guess_rstd(i, 1)
                    elif kind == "ln2T":
                        b = when_full(i, s)
                        copy(x_hi[:, s[1], :], bank[b][:, :]).then_inc(x2_hi.sem, 1)
                    elif kind == "ln1T" and not last:
                        b = when_full(i, s)
                        copy(x_hi[:, s[1], :], bank[b][:, :]).then_inc(x1_hi.sem, 1)
                    elif kind == "gate":
                        b = when_full(i, s)
                        copy(gate_log[0:GPAD, :], bank[b][0:GPAD, :]).then_inc(read[b], 1)
                    elif kind == "rbc":
                        b = when_full(i, s)
                        copy(r_bc[:, :], bank[b][:, :]).then_inc(read[b], 1)
                    elif kind == "fc1":
                        b = when_full(i, s)
                        copy(lat_hi[:, s[1], :], bank[b][:, :]).then_inc(lat_hi_done.sem, 1)
                    elif kind in ("exp", "up"):
                        n = t32_order(s)
                        b = when_full(i, s)
                        if kind == "up":
                            act.wait_ge(lo_ready.sem, lo_ready.at(i, KV * 16 + n + 1 - 2))
                            nc.scalar.activation(t32[:, n % 2, :], bank[b][:, :], ACT.Relu).then_inc(relu_done.sem, 1)
                        b, v = fill(i, s)
                        act.wait_ge(read[b], v + 1)
                        dst = moe_hi[:, s[1], :] if kind == "exp" else h_hi[:, s[1], :]
                        copy(dst, t32[:, n % 2, :]).then_inc(t_hi_done.sem, 1)
                    elif kind == "down" and s[2] == DC - 1:
                        for tt in range(TT):
                            b = when_full(i, ("down", s[1], tt))
                            copy(y[:, tt, s[1] * HALF:(s[1] + 1) * HALF], bank[b][:, :]).then_inc(read[b], 1)
                        if s[1] == 1:
                            guess_rstd(i, 2 if last else 3)

            over_blocks(act, body)

        @block.gpsimd
        def _(pool):
            def lo(out_, x32, hi):
                return nc.gpsimd.tensor_tensor(out_, x32, hi.bitcast(F32), ALU.subtract)

            def split_w(i, u):
                i, u = (i, u) if u < UNITS else (i + 1, u - UNITS)
                n = unit_dram(u)[1]
                pool.wait_ge(w_hi_done.sem, w_hi_done.at(i, u + 1))
                lo(w_lo[:, u % 2, 0:n], w_st[:, u % 2, 0:n], w_hi[:, u % 2, 0:n]).then_inc(w_ready.sem, 1)

            def split_c(i, kc):
                i, kc = (i, kc) if kc < KC else (i + 1, kc - KC)
                pool.wait_ge(c_hi_done.sem, c_hi_done.at(i, kc + 1))
                lo(c_lo[:, kc % 2, :], c_st[:, kc % 2, :], c_hi[:, kc % 2, :]).then_inc(c_ready.sem, 1)

            pool.sem_inc(out_stored.sem, out_stored.credit)
            for b in range(NBANK):
                pool.sem_inc(read[b], 1)
            nc.gpsimd.memset(ident[:, :], 0.0).then_inc(zeroed, 1)
            nc.gpsimd.memset(gate_w[:, :, :].bitcast(F32), 0.0).then_inc(zeroed, 1)
            pool.wait_ge(zeroed, 2)
            nc.gpsimd.affine_select(out=ident[:, :], in_=ident[:, :], compare_op=ALU.not_equal, fill=1.0, base=0,
                                    pattern=[[-1, P]], channel_multiplier=1).then_inc(ident_ready, 1)
            pool.wait_ge(gate_hi_done, 1)
            lo(gate_w[:, :, 32:32 + EXPERTS], gate_st[:, :, :], gate_w[:, :, 0:EXPERTS]).then_inc(gate_ready, 1)
            split_c(0, 0)
            split_w(0, 0)

            def body(i, last):
                for s in STEPS:
                    kind, u = s[0], unit_of(s)
                    if kind == "kv" and s[1] == 0 and s[2] + 1 < KC:
                        split_c(i, s[2] + 1)
                    if kind == "o" and s[1:] == (0, 0):
                        for t in range(2):
                            pool.wait_ge(o_hi_done.sem, o_hi_done.at(i, t + 1))
                            lo(o_lo[:, t, :], o32[:, t, :], o_hi[:, t, :]).then_inc(o_ready.sem, 1)
                    if u is not None and (u + 1 < UNITS or not last):
                        split_w(i, u + 1)
                    if kind == "o" and s[1] == 0:
                        for t in range(2 * s[2] + 2, min(2 * s[2] + 4, OT)):
                            pool.wait_ge(o_hi_done.sem, o_hi_done.at(i, t + 1))
                            lo(o_lo[:, t, :], o32[:, t, :], o_hi[:, t, :]).then_inc(o_ready.sem, 1)
                    if u == UNITS - 1 and not last:
                        split_c(i, KC)

                    if kind == "kv" and s[1:] == (0, KC - 1):
                        b, v = fill(i, ("kv", 0, 0))
                        pool.wait_ge(full[b], v)
                        waited(pool)
                        nc.gpsimd.memset(v_hi[:, :, :, :, HD:P].rearrange("p c t g d -> p (c t g) d").bitcast(F32),
                                         1.0).then_inc(ones_ready.sem, 1)
                    elif kind == "score":
                        for kt in range(4):
                            k = s[1] * 16 + s[2] * 4 + kt
                            b, v = fill(i, s + (kt,))
                            pool.wait_ge(read[b], v + 1)
                            lo(p_lo[:, k % PRING].rearrange("p b s -> p (b s)"), t32[:, k % 2, :],
                               p_hi[:, k % PRING].rearrange("p b s -> p (b s)")).then_inc(lo_ready.sem, 1)
                    elif kind == "gate":
                        b, v = fill(i, ("ln2T", KC - 1))
                        pool.wait_ge(full[b], v)
                        waited(pool)
                        nc.gpsimd.memset(gate_ones[:, :], 1.0).then_inc(ones_ready.sem, 1)
                    elif kind in ("exp", "up"):
                        n = t32_order(s)
                        pool.wait_ge(t_hi_done.sem, t_hi_done.at(i, n + 1))
                        hi, dst = (moe_hi, moe_lo) if kind == "exp" else (h_hi, h_lo)
                        lo(dst[:, s[1], :], t32[:, n % 2, :], hi[:, s[1], :]).then_inc(lo_ready.sem, 1)
                    elif kind == "down" and s[1:] == (0, 2):
                        pool.wait_ge(gb_loaded.sem, gb_loaded.at(i, 2))
                        pool.wait_ge(tanh_ready, 1)
                        pool.wait_ge(xn2_ready.sem, xn2_ready.at(i, TT))
                        waited(pool)
                        nc.gpsimd.tensor_scalar(bet[:, :], bet[:, :], tg[:, 1:2], None, ALU.mult)
                        nc.gpsimd.tensor_scalar(gam[:, :], gam[:, :], tg[:, 1:2], None,
                                                ALU.mult).then_inc(pool_chain.sem, 1)
                        pool.wait_ge(pool_chain.sem, pool_chain.at(i, 1))
                    elif kind == "down" and s[1] == 0 and 3 <= s[2] < 3 + TT:
                        tt = s[2] - 3
                        op = nc.gpsimd.tensor_tensor(x2[:, tt, :], x2[:, tt, :], bet[:, :], ALU.add)
                        if tt == TT - 1:
                            op.then_inc(gb_ready.sem, 1)

            over_blocks(pool, body)

        @block.vector
        def _(dve):
            v_ = nc.vector
            links = [0]

            def link(i, op):
                links[0] += 1
                op.then_inc(dve_chain.sem, 1)
                dve.wait_ge(dve_chain.sem, AHEAD_LINKS + dve_chain.at(i, links[0]) if i is not None else links[0])

            def when_full(i, job):
                b, v = fill(i, job)
                dve.wait_ge(full[b], v)
                return b

            def stats(src, tt, h):
                return v_.bn_stats(bn[:, tt, h, :], src[:, tt, h * HALF:(h + 1) * HALF])

            def mean_var(i, ki, k):
                waited(dve)
                for tt in range(TT):
                    op = v_.bn_aggr(mv[:, tt, :], bn[:, tt, :, :].rearrange("p a b -> p (a b)"))
                link(i, op)
                v_.tensor_scalar(var[:, :], mv[:, :, 1], EPS, None, ALU.add).then_inc(var_ready.sem, 1)
                dve.wait_ge(rstd_guess.sem, rstd_guess.at(ki, k))
                link(i, v_.tensor_tensor(newt[:, :], rstd0[:, :], rstd0[:, :], ALU.mult))
                link(i, v_.scalar_tensor_tensor(newt[:, :], newt[:, :], -0.5, var[:, :], ALU.mult, ALU.mult))
                link(i, v_.scalar_tensor_tensor(rstd[:, :], newt[:, :], 1.5, rstd0[:, :], ALU.add, ALU.mult))

            def layernorm(dst, src, tt):
                return v_.tensor_scalar(dst[:, tt, :], src[:, tt, :], mv[:, tt, 0:1], rstd[:, tt:tt + 1],
                                        ALU.subtract, ALU.mult)

            def lo(out_, x32, hi):
                return v_.tensor_tensor(out_, x32, hi.bitcast(F32), ALU.subtract)

            link(None, v_.memset(row_max[:, :], 0.0))
            dve.wait_ge(ident_ready, 1)
            link(None, v_.tensor_scalar(neg_mask[:, :], ident[0:GROUP, 0:GROUP], -1.0, None, ALU.mult))
            dve.wait_ge(tanh_ready, 1)
            for tt in range(TT):
                dve.wait_ge(x_loaded[tt].sem, 16)
                stats(rows, tt, 0)
                op = stats(rows, tt, 1)
            link(None, op)
            mean_var(None, 0, 0)
            for tt in range(TT):
                layernorm(rows, rows, tt).then_inc(xn_ready.sem, 1)
            for kc in range(KC):
                b = when_full("ahead", ("ln1T", kc))
                dve.wait_ge(x1_hi.sem, kc + 1)
                lo(x_lo[:, kc, :], bank[b][:, :], x_hi[:, kc, :]).then_inc(read[b], 1)
            assert links[0] == AHEAD_LINKS, links[0]

            def body(i, last):
                links[0] = 0
                for s in STEPS:
                    kind = s[0]
                    if kind == "kv" and s[2] == KC - 1:
                        src = s[1]
                        if src == 0:
                            when_full(i, ("kv", 0, 0))
                            v_.memset(k_hi[96:96 + GROUP].rearrange("p g b c s -> p (g b c s)").bitcast(F32), 1.0)
                        for t in range(HT):
                            b = when_full(i, ("kv", src, t))
                            dve.wait_ge(kv_hi.sem, kv_hi.at(i, src * (HT + TT) + t + 1))
                            lo(k_lo[0:96, t, :, src, :], bank[b][0:96, :].rearrange("p (b s) -> p b s", b=BPB),
                               k_hi[0:96, t, :, src, :])
                            lo(k_lo[32 * t:32 * t + 32, 3, :, src, :],
                               bank[b][96:128, :].rearrange("p (b s) -> p b s", b=BPB),
                               k_hi[32 * t:32 * t + 32, 3, :, src, :]).then_inc(read[b], 1)
                        for tt in range(TT):
                            b = when_full(i, ("kv", src, HT + tt))
                            dve.wait_ge(kv_hi.sem, kv_hi.at(i, src * (HT + TT) + HT + tt + 1))
                            lo(v_lo[:, src, tt, :, :], bank[b][:, 0:KV * HD].rearrange("p (g d) -> p g d", g=KV),
                               v_hi[:, src, tt, :, 0:HD]).then_inc(read[b], 1)
                    elif kind == "q":
                        g, t = s[1:]
                        b = when_full(i, s)
                        dve.wait_ge(q_hi_done.sem, q_hi_done.at(i, g * HT + t + 1))
                        lo(q_lo[g % 2][0:96, t, :], bank[b][0:96, :], q_hi[g % 2][0:96, t, :])
                        lo(q_lo[g % 2][32 * t:32 * t + 32, 3, :], bank[b][96:128, :],
                           q_hi[g % 2][32 * t:32 * t + 32, 3, :]).then_inc(read[b], 1)
                    elif kind == "max":
                        g, tt = s[1:]
                        if tt == 0 and g:
                            b, v = fill(i, ("maxT", g - 1))
                            dve.wait_ge(full[b], v)
                        for h in range(GROUP):
                            b = when_full(i, s + (h,))
                            v_.reduce_max(row_max[:, tt * GROUP + h:tt * GROUP + h + 1], bank[b][:, :],
                                          AX.X).then_inc(read[b], 1)
                    elif kind == "maxT":
                        g = s[1]
                        b = when_full(i, s)
                        v_.tensor_tensor(q_hi[g % 2][96:96 + GROUP, :, :],
                                         bank[b][0:GROUP, :].unsqueeze(1).broadcast_to([GROUP, GROUP, TOK]),
                                         neg_mask[:, :].unsqueeze(2).broadcast_to([GROUP, GROUP, TOK]),
                                         ALU.mult).then_inc(read[b], 1)
                    elif kind == "pv":
                        g, n = s[1:]
                        bt, pair = n // 2, n % 2
                        b = when_full(i, s)
                        acc = bank[b][:, :].rearrange("p (h s) -> p h s", h=2)
                        dve.wait_ge(inv_ready.sem, inv_ready.at(i, g * 4 + n + 1))
                        link(i, v_.tensor_tensor(neg_inv[:, :, :], acc[96:128], inv_guess[:, :, :], ALU.mult))
                        link(i, v_.scalar_tensor_tensor(neg_inv[:, :, :], neg_inv[:, :, :], 2.0, inv_guess[:, :, :],
                                                        ALU.subtract, ALU.mult))
                        o_t = o32[:, HT * g:HT * g + HT, :].rearrange("p t (b s) -> p t b s", b=BPB)
                        for j in range(HT):
                            r = slice(32 * j, 32 * j + 32)
                            if pair == 0:
                                op = v_.scalar_tensor_tensor(o_t[r, 0:2, bt, :], acc[r], -1.0, neg_inv[:, :, :],
                                                             ALU.mult, ALU.mult)
                            else:
                                v_.scalar_tensor_tensor(o_t[r, 2, bt, :], acc[r, 0, :], -1.0, neg_inv[:, 0, :],
                                                        ALU.mult, ALU.mult)
                                op = v_.scalar_tensor_tensor(o_t[96:128, j, bt, :], acc[r, 1, :], -1.0,
                                                             neg_inv[:, 1, :], ALU.mult, ALU.mult)
                        op.then_inc(read[b], 1)
                    elif kind == "o" and s[2] == OT // 2 - 1:
                        half = s[1]
                        dve.wait_ge(xres_loaded.sem, xres_loaded.at(i, 1))
                        for tt in range(TT):
                            b = when_full(i, ("o", half, tt))
                            xs = x2[:, tt, half * HALF:(half + 1) * HALF]
                            op = v_.scalar_tensor_tensor(xs, bank[b][:, :], tg[:, 0:1], xs, ALU.mult, ALU.add)
                            op.then_inc(read[b], 1)
                        for tt in range(TT):
                            b, v = fill(i, ("o", half, tt))
                            dve.wait_ge(read[b], v + 1)
                            op = stats(x2, tt, half)
                        if half == 1:
                            link(i, op)
                            dve.wait_ge(o_ready.sem, o_ready.at(i, OT))
                            mean_var(i, i, 1)
                            for tt in range(TT):
                                op = layernorm(rows, x2, tt)
                                op.then_inc(xn2_ready.sem, 1)
                    elif kind == "ln2T":
                        b = when_full(i, s)
                        dve.wait_ge(x2_hi.sem, x2_hi.at(i, s[1] + 1))
                        lo(x_lo[:, s[1], :], bank[b][:, :], x_hi[:, s[1], :]).then_inc(read[b], 1)
                    elif kind == "gateT":
                        b = when_full(i, s)
                        t4 = bank[b][:, :].rearrange("p (t e) -> p t e", t=TT)
                        link(i, v_.tensor_copy(logits[:, :, :], t4[:, :, 0:EXPERTS]))
                        v_.tensor_tensor(logits[:, :, :], logits[:, :, :], t4[:, :, 32:32 + EXPERTS],
                                         ALU.add).then_inc(read[b], 1)
                        b, v = fill(i, s)
                        dve.wait_ge(read[b], v + 1)
                        waited(dve)
                        for tt in range(TT):
                            op = v_.max(top8[:, tt, :], logits[:, tt, :])
                        link(i, op)
                        link(i, v_.tensor_tensor(r_sum[:, :], top8[:, :, 0], top8[:, :, 1], ALU.add))
                        for tt in range(TT):
                            op = v_.tensor_scalar(r_diag[:, tt * P:(tt + 1) * P], ident[:, :], r_sum[:, tt:tt + 1],
                                                  None, ALU.mult)
                        op.then_inc(diag_ready.sem, 1)
                    elif kind == "fc1":
                        b = when_full(i, s)
                        dve.wait_ge(lat_hi_done.sem, lat_hi_done.at(i, s[1] + 1))
                        lo(lat_lo[:, s[1], :], bank[b][:, :], lat_hi[:, s[1], :]).then_inc(read[b], 1)
                    elif kind == "exp":
                        n = t32_order(s)
                        b, v = fill(i, ("rbc",))
                        dve.wait_ge(read[b], v + 1)
                        b = when_full(i, s)
                        dve.wait_ge(lo_ready.sem, lo_ready.at(i, KV * 16 + n + 1 - 2))
                        v_.tensor_tensor(t32[:, n % 2, :], bank[b][:, :], r_bc[:, :], ALU.mult).then_inc(read[b], 1)
                    elif kind == "up":
                        n = t32_order(s)
                        b = when_full(i, s)
                        dve.wait_ge(relu_done.sem, relu_done.at(i, s[1] + 1))
                        v_.scalar_tensor_tensor(t32[:, n % 2, :], bank[b][:, :], 0.0, t32[:, n % 2, :],
                                                ALU.max, ALU.mult).then_inc(read[b], 1)
                    elif kind == "down" and s[1:] == (0, 0) and not last:
                        for tt in range(TT):
                            dve.wait_ge(x_loaded[tt].sem, x_loaded[tt].at(i + 1, 1))
                            stats(rows, tt, 0)
                            op = stats(rows, tt, 1)
                        link(i, op)
                        mean_var(i, i, 2)
                        for tt in range(TT):
                            layernorm(rows, rows, tt).then_inc(xn_ready.sem, 1)
                    elif kind == "ln1T" and not last:
                        b = when_full(i, s)
                        dve.wait_ge(x1_hi.sem, x1_hi.at(i + 1, s[1] + 1))
                        lo(x_lo[:, s[1], :], bank[b][:, :], x_hi[:, s[1], :]).then_inc(read[b], 1)
                    elif kind == "down" and s[2] == DC - 1:
                        for tt in range(TT):
                            b, v = fill(i, ("down", s[1], tt))
                            dve.wait_ge(read[b], v + 1)
                            op = stats(y, tt, s[1])
                        if s[1] == 1:
                            link(i, op)
                            mean_var(i, i, 2 if last else 3)
                            dve.wait_ge(gb_ready.sem, gb_ready.at(i, 1))
                            for tt in range(TT):
                                op = v_.scalar_tensor_tensor(y[:, tt, :], y[:, tt, :], mv[:, tt, 0:1], gam[:, :],
                                                             ALU.subtract, ALU.mult)
                            link(i, op)
                            for tt in range(TT):
                                v_.scalar_tensor_tensor(y[:, tt, :], y[:, tt, :], rstd[:, tt:tt + 1], x2[:, tt, :],
                                                        ALU.mult, ALU.add).then_inc(y_ready.sem, 1)
                assert last or links[0] == DVE_LINKS, links[0]

            over_blocks(dve, body)

        @block.tensor
        def _(pe):
            mm = nc.tensor.matmul

            def split_product(out_, w, wl, m, ml, first, final):
                mm(out_, w, m, start=first, stop=False)
                mm(out_, w, ml, start=False, stop=False)
                return mm(out_, wl, m, start=False, stop=final)

            def when_free(i, job):
                b, v = fill(i, job)
                pe.wait_ge(read[b], v)
                return b

            def when_read(i, job):
                b, v = fill(i, job)
                pe.wait_ge(read[b], v + 1)

            def transpose_rows(i, job, kc):
                b = when_free(i, job)
                for tt in range(TT):
                    op = nc.tensor.transpose(bank[b][:, tt * P:(tt + 1) * P], rows[:, tt, kc * P:(kc + 1) * P],
                                             ident[:, :])
                op.then_inc(full[b], 1)

            pe.wait_ge(ident_ready, 1)
            pe.wait_ge(xn_ready.sem, TT)
            for kc in range(KC):
                transpose_rows("ahead", ("ln1T", kc), kc)
            pe.wait_ge(gate_ready, 1)

            def body(i, last):
                for s in STEPS:
                    kind, u = s[0], unit_of(s)
                    if kind == "exp":
                        u = U_EXP + s[1] // 2
                    if u is not None:
                        pe.wait_ge(w_ready.sem, w_ready.at(i, u + 1))
                        wh, wl = w_hi[:, u % 2, :], w_lo[:, u % 2, :]
                    op = None
                    if kind == "kv":
                        src, kc = s[1:]
                        if src == 0:
                            pe.wait_ge(c_ready.sem, c_ready.at(i, kc + 1))
                            ah, al = c_hi[:, kc % 2, :], c_lo[:, kc % 2, :]
                        else:
                            ah, al = x_hi[:, kc, :], x_lo[:, kc, :]
                            if kc == 0:
                                b, _ = BANK[("ln1T", KC - 1)]
                                pe.wait_ge(read[b], i * FILLS[b] + (FILLS_AHEAD[b] + 1))
                        first, final = kc == 0, kc == KC - 1
                        for t in range(HT):
                            job = ("kv", src, t)
                            b = when_free(i, job) if first else fill(i, job)[0]
                            op = split_product(bank[b][:, :], wh[:, t * P:(t + 1) * P], wl[:, t * P:(t + 1) * P],
                                               ah, al, first, final)
                            if final:
                                op.then_inc(full[b], 1)
                        for tt in range(TT):
                            job = ("kv", src, HT + tt)
                            b = when_free(i, job) if first else fill(i, job)[0]
                            tok = slice(tt * P, (tt + 1) * P)
                            op = split_product(bank[b][:, 0:KV * HD], ah[:, tok], al[:, tok],
                                               wh[:, HT * P:KVW], wl[:, HT * P:KVW], first, final)
                            if final:
                                op.then_inc(full[b], 1)
                    elif kind in ("q", "fc1", "up"):
                        if kind == "fc1" and s[1] == 0:
                            when_read(i, ("ln2T", KC - 1))
                        b = when_free(i, s)
                        for kc in range(KC):
                            c = slice(kc * P, (kc + 1) * P)
                            op = split_product(bank[b][:, :], wh[:, c], wl[:, c], x_hi[:, kc, :], x_lo[:, kc, :],
                                               kc == 0, kc == KC - 1)
                        op.then_inc(full[b], 1)
                    elif kind == "exp":
                        if s[1] == 0:
                            when_read(i, ("fc1", LT - 1))
                        b = when_free(i, s)
                        for kc in range(LT):
                            at = ((s[1] % 2) * LT + kc) * P
                            op = split_product(bank[b][:, :], wh[:, at:at + P], wl[:, at:at + P],
                                               lat_hi[:, kc, :], lat_lo[:, kc, :], kc == 0, kc == LT - 1)
                        op.then_inc(full[b], 1)
                    elif kind == "max":
                        g, tt = s[1:]
                        if tt == 0:
                            when_read(i, ("kv", 1, HT + TT - 1))
                            when_read(i, ("q", g, HT - 1))
                        for h in range(GROUP):
                            b = when_free(i, s + (h,))
                            mm(bank[b][:, :], q_hi[g % 2][0:HD, h, tt * P:(tt + 1) * P],
                               k_hi[0:HD, g, tt // 2, :, :].rearrange("p c s -> p (c s)"),
                               start=True, stop=True).then_inc(full[b], 1)
                    elif kind == "maxT":
                        when_read(i, ("max", s[1], TT - 1, GROUP - 1))
                        b = when_free(i, s)
                        for tt in range(TT):
                            op = nc.tensor.transpose(bank[b][:, tt * P:(tt + 1) * P],
                                                     row_max[:, tt * GROUP:tt * GROUP + P], ident[:, :])
                        op.then_inc(full[b], 1)
                    elif kind == "score":
                        g, n = s[1:]
                        bt, pair = n // 2, n % 2
                        if n == 0:
                            pe.wait_ge(ones_ready.sem, ones_ready.at(i, 1))
                            when_read(i, ("maxT", g))
                        heads, tok = slice(2 * pair, 2 * pair + 2), slice(bt * SEQ, (bt + 1) * SEQ)
                        A = HD + GROUP
                        for kt in range(4):
                            b = when_free(i, s + (kt,))
                            keys = slice(kt % 2 * P, (kt % 2 + 1) * P)
                            mm(bank[b][:, :], k_hi[0:A, g, bt, kt // 2, keys], q_hi[g % 2][0:A, heads, tok],
                               start=True, stop=False)
                            mm(bank[b][:, :], k_hi[0:HD, g, bt, kt // 2, keys], q_lo[g % 2][0:HD, heads, tok],
                               start=False, stop=False)
                            mm(bank[b][:, :], k_lo[0:HD, g, bt, kt // 2, keys], q_hi[g % 2][0:HD, heads, tok],
                               start=False, stop=True).then_inc(full[b], 1)
                    elif kind == "pv":
                        g, n = s[1:]
                        b = when_free(i, s)
                        for kt in range(4):
                            k = g * 16 + n * 4 + kt
                            pe.wait_ge(lo_ready.sem, lo_ready.at(i, k + 1))
                            tt = n // 2 * 2 + kt % 2
                            ph, pl = (p[:, k % PRING].rearrange("p b s -> p (b s)") for p in (p_hi, p_lo))
                            mm(bank[b][:, :], v_hi[:, kt // 2, tt, g, :], ph, start=kt == 0, stop=False)
                            mm(bank[b][0:HD, :], v_lo[:, kt // 2, tt, g, :], ph, start=False, stop=False)
                            op = mm(bank[b][:, :], v_hi[:, kt // 2, tt, g, :], pl, start=False, stop=kt == 3)
                            if kt < 3:
                                op.then_inc(p_used.sem, 1)
                        op.then_inc(full[b], 1)
                    elif kind in ("o", "down"):
                        half, c = s[1:]
                        for e in range(2):
                            t = 2 * c + e
                            if kind == "o":
                                ah, al = o_hi[:, t, :], o_lo[:, t, :]
                                if half == 0:
                                    pe.wait_ge(o_ready.sem, o_ready.at(i, t + 1))
                                first, final = t == 0, t == OT - 1
                            else:
                                moe = t < LT
                                hi, lo = (moe_hi, moe_lo) if moe else (h_hi, h_lo)
                                ah, al = (hi[:, t, :], lo[:, t, :]) if moe else (hi[:, t - LT, :], lo[:, t - LT, :])
                                n = t32_order(("exp", t) if moe else ("up", t - LT))
                                if half == 0:
                                    pe.wait_ge(lo_ready.sem, lo_ready.at(i, KV * 16 + n + 1))
                                first, final = t == 0, t == LT + UT - 1
                            for tt in range(TT):
                                job = (kind, half, tt)
                                b = when_free(i, job) if first else fill(i, job)[0]
                                tok, n = slice(tt * P, (tt + 1) * P), slice(e * HALF, (e + 1) * HALF)
                                op = split_product(bank[b][:, :], ah[:, tok], al[:, tok], wh[:, n], wl[:, n],
                                                   first, final)
                                if final:
                                    op.then_inc(full[b], 1)
                    elif kind == "ln2T":
                        if s[1] == 0:
                            pe.wait_ge(xn2_ready.sem, xn2_ready.at(i, TT))
                        transpose_rows(i, s, s[1])
                    elif kind == "ln1T" and not last:
                        if s[1] == 0:
                            pe.wait_ge(xn_ready.sem, xn_ready.at(i + 1, TT))
                        transpose_rows(i, s, s[1])
                    elif kind == "gate":
                        b = when_free(i, s)
                        for kc in range(KC):
                            when_read(i, ("ln2T", kc))
                            mm(bank[b][0:GPAD, :], gate_w[:, kc, :], x_hi[:, kc, :], start=kc == 0, stop=False)
                            op = mm(bank[b][0:GPAD, :], gate_w[:, kc, :], x_lo[:, kc, :], start=False,
                                    stop=kc == KC - 1)
                        op.then_inc(full[b], 1)
                    elif kind == "gateT":
                        when_read(i, ("gate",))
                        b = when_free(i, s)
                        for tt in range(TT):
                            op = nc.tensor.transpose(bank[b][:, tt * P:tt * P + GPAD],
                                                     gate_log[0:GPAD, tt * P:(tt + 1) * P], ident[0:GPAD, 0:GPAD])
                        op.then_inc(full[b], 1)
                    elif kind == "rbc":
                        pe.wait_ge(ones_ready.sem, ones_ready.at(i, 2))
                        pe.wait_ge(diag_ready.sem, diag_ready.at(i, 1))
                        b = when_free(i, s)
                        mm(bank[b][:, :], gate_ones[:, :], r_diag[:, :], start=True, stop=True).then_inc(full[b], 1)
                    if u in COUNTED:
                        op.then_inc(w_used.sem, 1)

            over_blocks(pe, body)


def kernel(x, ctx_4096, g_xattn, g_ffn, L0_xattn_Wq, L0_xattn_Wk, L0_xattn_Wv, L0_xattn_Wo, L0_ffn_gate_w,
           L0_ffn_up_w, L0_ffn_down_w, L0_ffn_fc1_w, L0_ffn_fc2_w, L0_ffn_expert_w, L0_ffn_ln_gamma, L0_ffn_ln_beta):
    import numpy as np
    import concourse.bacc as bacc
    from concourse.bass_utils import run_bass_kernel_spmd

    x, ctx, Wq, Wk, Wv, Wo, gate, up, down, fc1, fc2, expert, gamma, beta = (np.asarray(a) for a in (
        x, ctx_4096, L0_xattn_Wq, L0_xattn_Wk, L0_xattn_Wv, L0_xattn_Wo, L0_ffn_gate_w, L0_ffn_up_w, L0_ffn_down_w,
        L0_ffn_fc1_w, L0_ffn_fc2_w, L0_ffn_expert_w, L0_ffn_ln_gamma, L0_ffn_ln_beta))
    group = np.concatenate([np.r_[t * HD:(t + 1) * HD, 3 * HD + 32 * t:3 * HD + 32 * t + 32] for t in range(HT)])
    order = np.concatenate([g * GROUP * HD + group for g in range(KV)])

    def stationary(w, chunks, tiles=1):
        n = w.shape[1] // (P * tiles)
        return w.reshape(chunks, P, n, tiles, P).transpose(2, 1, 3, 0, 4).reshape(n, P, tiles * chunks * P)

    def moving(w):
        n = w.shape[0] // (2 * P)
        return w.reshape(n, 2, P, 2, HALF).transpose(3, 0, 2, 1, 4).reshape(2 * n, P, DIM)

    arrays = {
        "x": x.reshape(-1, DIM),
        "ctxT": ctx.reshape(BLOCKS, TOK, KC, P).transpose(0, 2, 3, 1),
        "g_x": g_xattn, "g_f": g_ffn,
        "w_kv": np.concatenate([Wk.T[:, group], Wv.T], axis=1).reshape(KC, P, KVW),
        "w_q": stationary(Wq.T[:, order], KC),
        "w_o": moving(Wo.T[order]),
        "w_fc1": stationary(fc1, KC),
        "w_exp": stationary(expert, LT, 2),
        "w_up": stationary(up, KC),
        "w_down": moving(np.concatenate([fc2, down])),
        "w_gate": gate.reshape(KC, P, EXPERTS).transpose(1, 0, 2),
        "gamma": gamma, "beta": beta,
    }
    arrays = {f"in_{k}": np.ascontiguousarray(np.asarray(a)) for k, a in arrays.items()}
    nc = bacc.Bacc("TRN2", target_bir_lowering=False, num_devices=1)
    args = [nc.dram_tensor(k, a.shape, F32, kind="ExternalInput").ap() for k, a in arrays.items()]
    args.append(nc.dram_tensor("out", (BATCH * SEQ, DIM), F32, kind="ExternalOutput").ap())
    layer_kernel(nc, *args)
    r = run_bass_kernel_spmd(nc, [arrays], core_ids=[0])
    return r.results[0]["out"].reshape(BATCH, SEQ, DIM)
```

```python
from contextlib import ExitStack

import concourse.bass as bass
from concourse import mybir
from concourse.alu_op_type import AluOpType as ALU

F32 = mybir.dt.float32
F32R = mybir.dt.float32r
ACT = mybir.ActivationFunctionType
AX = mybir.AxisListType

BATCH, SEQ, DIM = 8, 256, 1024
KV, GROUP, HD = 4, 4, 96
INT, LAT, EXPERTS = 2048, 512, 8
EPS = 1e-5
SCALE = float(HD) ** -0.5
P = 128
TOK = 512
BLOCKS = BATCH * SEQ // TOK
BPB = TOK // SEQ
TT = TOK // P
KC = DIM // P
HT = 3
OT = KV * HT
UT = INT // P
LT = LAT // P
HALF = DIM // 2
KVW = HT * P + KV * HD
GPAD = 66
DC = (LT + UT) // 2
MXW = TT * GROUP + P - GROUP

U_CTX = 0
U_Q00 = U_CTX + KC
U_X = U_Q00 + 1
U_Q = U_X + KC - 1
U_O = U_Q + KV * HT
U_FC1 = U_O + 2 * (OT // 2)
U_UP0 = U_FC1 + LT
U_EXP = U_UP0 + 2
U_UP2 = U_EXP + LT // 2
U_DOWN = U_UP2 + UT - 2
UNITS = U_DOWN + 2 * DC
assert UNITS % 2 == 0
UNIT_UP = [U_UP0, U_UP0 + 1] + [U_UP2 + j for j in range(UT - 2)]

EARLY = 4
PRING = 6
NBANK = 8


def steps_main():
    s = [("kv", 0, kc) for kc in range(KC)] + [("q", 0, 0)] + [("kv", 1, kc) for kc in range(KC)]
    s += [("q", 0, 1), ("max", 0, 0), ("max", 0, 1), ("q", 0, 2), ("max", 0, 2), ("max", 0, 3), ("q", 1, 0),
          ("maxT", 0), ("q", 1, 1)]
    for g in range(KV):
        n = g + 1
        order = [("score", g, 0), ("q", n, 0), ("score", g, 1), ("max", n, 0), ("pv", g, 0), ("q", n, 1),
                 ("max", n, 1), ("pv", g, 1), ("q", n, 2), ("score", g, 2), ("max", n, 2), ("score", g, 3),
                 ("max", n, 3), ("pv", g, 2), ("maxT", n), ("pv", g, 3)]
        s += [x for x in order if (x[1] == g or n < KV) and x not in s]
    s += [("o", h, c) for h in range(2) for c in range(OT // 2)]
    s += [("ln2T", kc) for kc in range(KC)]
    s += [("gate",), ("fc1", 0), ("gateT",), ("fc1", 1), ("fc1", 2), ("rbc",), ("fc1", 3), ("up", 0), ("up", 1)]
    s += [("exp", j) for j in range(LT)] + [("up", j) for j in range(2, UT)]
    for c in range(DC):
        s += [("down", 0, c)]
        if 2 <= c < KC + 2:
            s += [("ln1T", c - 2)]
    s += [("down", 1, c) for c in range(DC)]
    return s


STEPS = steps_main()


def bank_plan():
    jobs = []
    for s in STEPS:
        if s[0] == "kv" and s[2] == 0:
            jobs += [("kv", s[1], t) for t in range(HT + TT)]
        elif s[0] == "max":
            jobs += [("max", s[1], s[2], tt) for tt in range(TT)]
        elif s[0] == "score":
            jobs += [("score", s[1], s[2], kt) for kt in range(4)]
        elif s[0] == "o" and s[2] == 0:
            jobs += [("o", s[1], tt) for tt in range(TT)]
        elif s[0] in ("q", "maxT", "pv", "ln2T", "gate", "gateT", "rbc", "fc1", "exp", "up", "ln1T"):
            jobs += [s]
        elif s[0] == "down" and s[2] == 0:
            jobs += [("down", s[1], tt) for tt in range(TT)]
    plan, fills, n = {}, [0] * NBANK, 0
    for j in jobs:
        if j[0] == "down":
            b = 4 * j[1] + j[2]
        elif j[0] == "ln1T":
            b = 4 + j[1] % 4
        else:
            b, n = n % NBANK, n + 1
        fills[b] += 1
        plan[j] = (b, fills[b])
    return plan, fills


def t32_order(s):
    return s[1] if s[0] == "up" and s[1] < 2 else 2 + s[1] if s[0] == "exp" else LT + s[1]


def vector_steps():
    s = list(STEPS)
    for n in range(1, KV):
        a, b = s.index(("pv", n - 1, 2)), s.index(("maxT", n))
        assert b == a + 1
        s[a], s[b] = s[b], s[a]
    return s


VECTOR_STEPS = vector_steps()
BANK, FILLS = bank_plan()
MEAN_LINKS = 4
AHEAD_LINKS = 3 + MEAN_LINKS
DVE_LINKS = 2 * KV * 4 + 3 * (1 + MEAN_LINKS) + 1 + 3
FILLS_AHEAD = [2 if b >= 4 else 0 for b in range(NBANK)]


def fill(block, job):
    b, k = BANK[job]
    if isinstance(block, str):
        return b, 1 + job[1] // 4
    if isinstance(block, int) and block == BLOCKS - 1 and job[:2] == ("down", 1):
        k -= KC // 4
    return b, block * FILLS[b] + (FILLS_AHEAD[b] + k)


def unit_of(s):
    if s[0] == "kv":
        return (U_CTX, U_X)[s[1]] + s[2]
    if s[0] == "q":
        return U_Q + s[1] * HT + s[2] if s[1:] != (0, 0) else U_Q00
    if s[0] == "o":
        return U_O + s[1] * (OT // 2) + s[2]
    if s[0] == "fc1":
        return U_FC1 + s[1]
    if s[0] == "exp" and s[1] % 2 == 0:
        return U_EXP + s[1] // 2
    if s[0] == "up":
        return UNIT_UP[s[1]]
    if s[0] == "down":
        return U_DOWN + s[1] * DC + s[2]
    return None


def unit_ends():
    ends = {}
    for s in STEPS:
        u = unit_of(s)
        if s[0] in ("q", "fc1", "up"):
            ends[u] = s
        elif s[0] == "exp" and s[1] % 2:
            ends[U_EXP + s[1] // 2] = s
        elif s[0] == "kv" and s[2] == KC - 1:
            ends[u] = ("kv", s[1], HT + TT - 1)
        elif s[0] == "o" and s[2] == OT // 2 - 1:
            ends[u] = ("o", s[1], TT - 1)
        elif s[0] == "down" and s[2] == DC - 1:
            ends[u] = ("down", s[1], TT - 1)
    return ends


ENDS = unit_ends()
COUNTED = [u for u in range(UNITS) if u not in ENDS]


class Count:

    def __init__(self, sem, per, credit=0, step=1):
        self.sem, self.per, self.credit, self.step = sem, per, credit, step

    def at(self, block, k):
        return block * (self.per * self.step) + (self.credit + k * self.step)


def layer_kernel(nc, x, ctxT, g_x, g_f, w_kv, w_q, w_o, w_fc1, w_exp, w_up, w_down, w_gate, gamma, beta, out):
    ctx = ExitStack()
    with ctx:
        sem = lambda name: ctx.enter_context(nc.semaphore(name))

        base = (nc.sbuf_base + 31) // 32 * 32
        top = [base]

        def region(size):
            at = top[0]
            top[0] += (size + 31) // 32 * 32
            return at

        def place(name, shape, dtype, at):
            return nc.alloc_sbuf_tensor_at(name, shape, dtype, offset=at)

        K4 = 4096
        r_x = region(8 * K4)
        r_kv = region(15 * K4)
        r_p = region(6 * K4)
        r_t32 = region(K4)
        r_o32 = region(6 * K4)
        r_qa = region(4 * K4)
        r_qb = region(4 * K4)
        r_ws = region(2 * K4)
        r_wh = region(2 * K4)
        r_wl = region(2 * K4)

        x_hi = place("x_hi", [P, KC, TOK], F32R, r_x)
        x_lo = place("x_lo", [P, KC, TOK], F32R, r_x + 4 * K4)
        k_hi = place("k_hi", [P, KV, BPB, 2, SEQ], F32R, r_kv)
        k_lo = place("k_lo", [P, KV, BPB, 2, SEQ], F32R, r_kv + 4 * K4)
        v_hi = place("v_hi", [P, 2, TT, KV, P], F32R, r_kv + 8 * K4)
        v_lo = place("v_lo", [P, 2, TT, KV, HD], F32R, r_kv + 12 * K4)
        o_hi = place("o_hi", [P, OT - EARLY, TOK], F32R, r_kv)
        o_lo = place("o_lo", [P, OT - EARLY, TOK], F32R, r_kv + 4 * K4)
        oe_hi = place("oe_hi", [P, EARLY, TOK], F32R, r_qb)
        oe_lo = place("oe_lo", [P, EARLY, TOK], F32R, r_qb + 2 * K4)
        h_hi = place("h_hi", [P, UT, TOK], F32R, r_kv)
        h_lo = place("h_lo", [P, UT, TOK], F32R, r_kv + 8 * K4)
        p_hi = place("p_hi", [P, PRING, 2, SEQ], F32R, r_p)
        p_lo = place("p_lo", [P, PRING, 2, SEQ], F32R, r_p + 3 * K4)
        x2 = place("x2", [P, TT, DIM], F32, r_p + K4)
        t32 = place("t32", [P, 2, TOK], F32, r_t32)
        o32 = place("o32", [P, OT, TOK], F32, r_o32)
        rows = place("rows", [P, TT, DIM], F32, r_o32)
        gate_log = place("gate_log", [P, TOK], F32, r_o32)
        r_diag = place("r_diag", [P, TOK], F32, r_o32 + K4)
        r_bc = place("r_bc", [P, TOK], F32, r_o32 + 2 * K4)
        gate_ones = place("gate_ones", [P, P], F32, r_o32 + 3 * K4)
        gam = place("gam", [P, DIM], F32, r_o32 + 4 * K4)
        bet = place("bet", [P, DIM], F32, r_o32 + 5 * K4)
        qa_hi = place("qa_hi", [P, GROUP, TOK], F32R, r_qa)
        qa_lo = place("qa_lo", [P, GROUP, TOK], F32R, r_qa + 2 * K4)
        lat_hi = place("lat_hi", [P, LT, TOK], F32R, r_qa)
        lat_lo = place("lat_lo", [P, LT, TOK], F32R, r_qa + 2 * K4)
        y = place("y", [P, TT, DIM], F32, r_qa)
        qb_hi = place("qb_hi", [P, GROUP, TOK], F32R, r_qb)
        qb_lo = place("qb_lo", [P, GROUP, TOK], F32R, r_qb + 2 * K4)
        c_st = place("c_st", [P, 2, TOK], F32, r_qb)
        c_hi = place("c_hi", [P, 2, TOK], F32R, r_qb + K4)
        c_lo = place("c_lo", [P, 2, TOK], F32R, r_qb + 2 * K4)
        moe_hi = place("moe_hi", [P, LT, TOK], F32R, r_qb)
        moe_lo = place("moe_lo", [P, LT, TOK], F32R, r_qb + 2 * K4)
        w_st = place("w_st", [P, 2, DIM], F32, r_ws)
        w_hi = place("w_hi", [P, 2, DIM], F32R, r_wh)
        w_lo = place("w_lo", [P, 2, DIM], F32R, r_wl)
        ident = place("ident", [P, P], F32, region(4 * P))
        gate_w = place("gate_w", [P, KC, GPAD], F32R, region(4 * KC * GPAD))
        inv_guess = place("inv_guess", [64, 2, SEQ], F32, region(4 * TOK))
        neg_inv = place("neg_inv", [64, 2, SEQ], F32, region(4 * TOK))
        gate_st = place("gate_st", [P, KC, EXPERTS], F32, r_t32)
        row_max = place("row_max", [P, MXW], F32, region(4 * MXW))
        neg_mask = place("neg_mask", [GROUP, GROUP], F32, region(32))
        bn = place("bn", [P, TT, 2, 6], F32, region(192))
        mv = place("mv", [P, TT, 2], F32, region(32))
        var = place("var", [P, TT], F32, region(32))
        rstd0 = place("rstd0", [P, TT], F32, region(32))
        newt = place("newt", [P, TT], F32, region(32))
        rstd = place("rstd", [P, TT], F32, region(32))
        logits = place("logits", [P, TT, EXPERTS], F32, region(128))
        top8 = place("top8", [P, TT, EXPERTS], F32, region(128))
        r_sum = place("r_sum", [P, TT], F32, region(32))
        tg = place("tg", [P, 2], F32, region(32))
        assert top[0] <= nc.sbuf_usable_end, top[0] - nc.sbuf_usable_end
        o_part = lambda hi, t: ((oe_hi if hi else oe_lo)[:, t, :] if t < EARLY else
                                (o_hi if hi else o_lo)[:, t - EARLY, :])
        q_hi, q_lo = [qb_hi, qa_hi], [qb_lo, qa_lo]

        bank = [ctx.enter_context(nc.psum_tensor(f"bank{b}", [P, TOK], F32)) for b in range(NBANK)]

        full = [sem(f"bank_full{b}") for b in range(NBANK)]
        read = [sem(f"bank_read{b}") for b in range(NBANK)]
        w_loaded = [Count(sem(f"w_loaded{s}"), UNITS // 2, step=16) for s in range(2)]
        w_hi_done = Count(sem("w_hi_done"), UNITS)
        w_ready = Count(sem("w_ready"), UNITS)
        w_used = Count(sem("w_used"), len(COUNTED))
        c_loaded = [Count(sem(f"c_loaded{s}"), KC // 2, step=16) for s in range(2)]
        c_hi_done = Count(sem("c_hi_done"), KC)
        c_ready = Count(sem("c_ready"), KC)
        x_loaded = [Count(sem(f"x_loaded{t}"), 1, step=16) for t in range(TT)]
        xn_ready = Count(sem("xn_ready"), TT)
        xn2_ready = Count(sem("xn2_ready"), TT)
        x1_hi = Count(sem("x1_hi"), KC)
        x2_hi = Count(sem("x2_hi"), KC)
        kv_hi = Count(sem("kv_hi"), 2 * (HT + TT))
        ones_ready = Count(sem("ones_ready"), 2)
        q_hi_done = Count(sem("q_hi_done"), KV * HT)
        p_used = Count(sem("p_used"), KV * 4 * 3)
        lo_ready = Count(sem("lo_ready"), KV * 16 + LT + UT)
        ln_done = Count(sem("ln_done"), KV * 4)
        inv_ready = Count(sem("inv_ready"), KV * 4)
        o_hi_done = Count(sem("o_hi_done"), OT)
        oe_ready = Count(sem("oe_ready"), EARLY)
        o_ready = Count(sem("o_ready"), OT - EARLY)
        xres_loaded = Count(sem("xres_loaded"), 1, step=16)
        diag_ready = Count(sem("diag_ready"), 1)
        lat_hi_done = Count(sem("lat_hi_done"), LT)
        relu_done = Count(sem("relu_done"), UT)
        t_hi_done = Count(sem("t_hi_done"), LT + UT)
        gb_loaded = Count(sem("gb_loaded"), 2, step=16)
        gb_ready = Count(sem("gb_ready"), 1)
        var_ready = Count(sem("var_ready"), 3, credit=1)
        rstd_guess = Count(sem("rstd_guess"), 3, credit=1)
        lnvar_done = Count(sem("lnvar_done"), 3, credit=1)
        y_ready = Count(sem("y_ready"), TT)
        out_stored = Count(sem("out_stored"), TT, credit=1, step=16)
        small_loaded, tanh_ready, gate_hi_done = sem("small_loaded"), sem("tanh_ready"), sem("gate_hi_done")
        zeroed, ident_ready = sem("zeroed"), sem("ident_ready")
        gate_ready = sem("gate_ready")
        dve_chain = Count(sem("dve_chain"), DVE_LINKS)
        waits_ended = sem("waits_ended")
        pool_chain = Count(sem("pool_chain"), 1)

        x_rows = x.rearrange("(i t p) d -> i t p d", t=TT, p=P)
        out_rows = out.rearrange("(i t p) d -> i t p d", t=TT, p=P)
        block = ctx.enter_context(nc.Block())

        def waited(eng):
            eng.sem_inc(waits_ended, 1)

        def over_blocks(eng, body):
            with eng.Fori(0, BLOCKS - 1) as i:
                body(i, False)
            body(BLOCKS - 1, True)

        def unit_dram(u):
            if u == U_Q00:
                return w_q[0], DIM
            if u <= U_Q:
                return w_kv[u - U_CTX if u < U_Q00 else u - U_X], KVW
            if u < U_O:
                return w_q[u - U_Q], DIM
            if u < U_FC1:
                return w_o[u - U_O], DIM
            if u < U_UP0:
                return w_fc1[u - U_FC1], DIM
            if U_EXP <= u < U_UP2:
                return w_exp[u - U_EXP], DIM
            if u < U_DOWN:
                return w_up[UNIT_UP.index(u)], DIM
            return w_down[u - U_DOWN], DIM

        def unit_used(eng, i, u):
            if u in ENDS:
                b, v = fill(i, ENDS[u])
                eng.wait_ge(full[b], v)
            else:
                eng.wait_ge(w_used.sem, w_used.at(i, COUNTED.index(u) + 1))

        def may_split(u, last):
            return u < UNITS or not last

        @block.sync
        def _(sp):
            def load_unit(i, u, ahead=None):
                src, n = unit_dram(u)
                if ahead is None:
                    sp.wait_ge(w_ready.sem, w_ready.at(i, u + 1 - 2))
                sp.dma_start(w_st[:, u % 2, 0:n], src).then_inc(w_loaded[u % 2].sem, 16)

            def load_ctx(i, kc):
                if kc >= 2:
                    sp.wait_ge(c_ready.sem, c_ready.at(i, kc + 1 - 2))
                    waited(sp)
                sp.dma_start(c_st[:, kc % 2, :], ctxT[i, kc]).then_inc(c_loaded[kc % 2].sem, 16)

            def load_rows(i):
                for tt in range(TT):
                    sp.dma_start(rows[:, tt, :], x_rows[i, tt]).then_inc(x_loaded[tt].sem, 16)

            load_rows(0)
            sp.dma_start(tg[:, 0:1], g_x.partition_broadcast(P)).then_inc(small_loaded, 16)
            sp.dma_start(tg[:, 1:2], g_f.partition_broadcast(P)).then_inc(small_loaded, 16)
            sp.dma_start(gate_st[:, :, :], w_gate).then_inc(small_loaded, 16)
            load_ctx(0, 0)
            load_unit(0, 0, ahead=True)
            load_ctx(0, 1)
            load_unit(0, 1, ahead=True)
            HEAD = KC
            for u in range(2, HEAD):
                load_unit(0, u)
                load_ctx(0, u)

            def store(i, tt):
                sp.wait_ge(y_ready.sem, y_ready.at(i, tt + 1))
                waited(sp)
                sp.dma_start(out_rows[i, tt], y[:, tt, :]).then_inc(out_stored.sem, 16)

            def body(i, last):
                for u in range(HEAD, UNITS):
                    load_unit(i, u)
                    if u == U_O + 2:
                        b, v = fill(i, ("pv", KV - 1, 3))
                        sp.wait_ge(full[b], v)
                        waited(sp)
                        sp.dma_start(x2[:, :, :], x_rows[i].rearrange("t p d -> p t d")).then_inc(xres_loaded.sem, 16)
                    if u == U_FC1 - 2:
                        sp.wait_ge(o_ready.sem, o_ready.at(i, OT - EARLY))
                        sp.dma_start(gam[:, :], gamma.partition_broadcast(P)).then_inc(gb_loaded.sem, 16)
                        sp.dma_start(bet[:, :], beta.partition_broadcast(P)).then_inc(gb_loaded.sem, 16)
                    if u == U_DOWN - 4 and not last:
                        b, v = fill(i, ("exp", LT - 1))
                        sp.wait_ge(read[b], v + 1)
                        waited(sp)
                        load_rows(i + 1)
                if not last:
                    unit_used(sp, i, UNITS - 4)
                    waited(sp)
                    for u in range(HEAD):
                        load_ctx(i + 1, u)
                        load_unit(i + 1, u)
                        if u >= HEAD - TT:
                            store(i, u - (HEAD - TT))
                else:
                    for tt in range(TT):
                        store(i, tt)
                    sp.wait_ge(out_stored.sem, out_stored.at(i, TT))

            over_blocks(sp, body)

        @block.scalar
        def _(act):
            copy = lambda o, i_: nc.scalar.activation(o, i_, ACT.Copy)

            def split_w(i, u, ahead=None):
                n = unit_dram(u % UNITS)[1]
                if ahead is None:
                    unit_used(act, i, u - 2)
                i, u = (i, u) if u < UNITS else (i + 1, u - UNITS)
                act.wait_ge(w_loaded[u % 2].sem, w_loaded[u % 2].at(i, u // 2 + 1))
                copy(w_hi[:, u % 2, 0:n], w_st[:, u % 2, 0:n]).then_inc(w_hi_done.sem, 1)

            def split_c(i, kc):
                act.wait_ge(c_loaded[kc % 2].sem, c_loaded[kc % 2].at(i, kc // 2 + 1))
                if kc >= 2:
                    unit_used(act, i, U_CTX + kc - 2)
                copy(c_hi[:, kc % 2, :], c_st[:, kc % 2, :]).then_inc(c_hi_done.sem, 1)

            def when_full(i, job):
                b, v = fill(i, job)
                act.wait_ge(full[b], v)
                return b

            def prob_used(i, k):
                if k % 4 == 3:
                    when_full(i, ("pv", k // 16, k // 4 % 4))
                else:
                    act.wait_ge(p_used.sem, p_used.at(i, k // 4 * 3 + k % 4 + 1))

            def guess_rstd(i, k):
                act.wait_ge(var_ready.sem, var_ready.at(i, k))
                nc.scalar.activation(rstd0[:, :], var[:, :], ACT.Ln).then_inc(lnvar_done.sem, 1)
                act.wait_ge(lnvar_done.sem, lnvar_done.at(i, k))
                nc.scalar.activation(rstd0[:, :], rstd0[:, :], ACT.Exp, scale=-0.5).then_inc(rstd_guess.sem, 1)

            act.wait_ge(small_loaded, 48)
            nc.scalar.activation(tg[:, :], tg[:, :], ACT.Tanh).then_inc(tanh_ready, 1)
            act.preload_act_table_set("natural_log_exp_and_others")
            act.wait_ge(zeroed, 2)
            copy(gate_w[:, :, 0:EXPERTS], gate_st[:, :, :]).then_inc(gate_hi_done, 1)
            guess_rstd(0, 0)
            for n in range(2):
                split_c(0, n)
                split_w(0, n, ahead=True)
            for kc in range(KC):
                b = when_full("ahead", ("ln1T", kc))
                copy(x_hi[:, kc, :], bank[b][:, :]).then_inc(x1_hi.sem, 1)

            def body(i, last):
                for s in STEPS:
                    kind, u = s[0], unit_of(s)
                    if kind == "o" and s[1:] == (0, 0):
                        when_full(i, ("pv", KV - 1, 3))
                    if kind == "o" and s[1] == 0:
                        for t in range(EARLY + 3 * s[2], min(EARLY + 3 * s[2] + 3, OT)):
                            if t == HT * (KV - 1):
                                b, v = fill(i, ("pv", KV - 1, 3))
                                act.wait_ge(read[b], v + 1)
                            copy(o_part(True, t), o32[:, t, :]).then_inc(o_hi_done.sem, 1)

                    if kind == "kv" and s[2] == KC - 1:
                        src = s[1]
                        for t in range(HT):
                            b = when_full(i, ("kv", src, t))
                            copy(k_hi[0:96, t, :, src, :], bank[b][0:96, :].rearrange("p (b s) -> p b s", b=BPB))
                            copy(k_hi[32 * t:32 * t + 32, 3, :, src, :],
                                 bank[b][96:128, :].rearrange("p (b s) -> p b s", b=BPB)).then_inc(kv_hi.sem, 1)
                        for tt in range(TT):
                            b = when_full(i, ("kv", src, HT + tt))
                            copy(v_hi[:, src, tt, :, 0:HD],
                                 bank[b][:, 0:KV * HD].rearrange("p (g d) -> p g d", g=KV)).then_inc(kv_hi.sem, 1)
                    elif kind == "q":
                        g, t = s[1:]
                        if (g, t) == (1, 0):
                            act.wait_ge(out_stored.sem, out_stored.at(i, 0))
                        b = when_full(i, s)
                        copy(q_hi[g % 2][0:96, t, :], bank[b][0:96, :])
                        copy(q_hi[g % 2][32 * t:32 * t + 32, 3, :], bank[b][96:128, :]).then_inc(q_hi_done.sem, 1)
                    elif kind == "score":
                        g, n = s[1:]
                        if (g, n) == (0, 0):
                            act.wait_ge(out_stored.sem, out_stored.at(i, 0))
                        for kt in range(4):
                            k = g * 16 + n * 4 + kt
                            b = when_full(i, s + (kt,))
                            if k >= 2:
                                act.wait_ge(lo_ready.sem, lo_ready.at(i, k + 1 - 2))
                            nc.scalar.activation(t32[:, k % 2, :], bank[b][:, :], ACT.Exp, scale=SCALE)
                            if k >= PRING:
                                prob_used(i, k - PRING)
                            nc.scalar.activation(p_hi[:, k % PRING].rearrange("p b s -> p (b s)"), bank[b][:, :],
                                                 ACT.Exp, scale=SCALE).then_inc(read[b], 1)
                    elif kind == "pv":
                        n = s[1] * 4 + s[2]
                        if n >= 2:
                            b, v = fill(i, ("pv", (n - 2) // 4, (n - 2) % 4))
                            act.wait_ge(read[b], v + 1)
                        b = when_full(i, s)
                        slot = inv_guess[32 * (n % 2):32 * (n % 2) + 32]
                        nc.scalar.activation(slot, bank[b][96:128, :].rearrange("p (h s) -> p h s", h=2),
                                             ACT.Ln).then_inc(ln_done.sem, 1)
                        act.wait_ge(ln_done.sem, ln_done.at(i, n + 1))
                        nc.scalar.activation(slot, slot, ACT.Exp, scale=-1.0).then_inc(inv_ready.sem, 1)
                        if s[1:] == (KV - 1, 0):
                            for t in range(EARLY):
                                copy(o_part(True, t), o32[:, t, :]).then_inc(o_hi_done.sem, 1)
                    elif kind == "ln2T":
                        b = when_full(i, s)
                        copy(x_hi[:, s[1], :], bank[b][:, :]).then_inc(x2_hi.sem, 1)
                    elif kind == "ln1T" and not last:
                        b = when_full(i, s)
                        copy(x_hi[:, s[1], :], bank[b][:, :]).then_inc(x1_hi.sem, 1)
                    elif kind == "gate":
                        b = when_full(i, s)
                        copy(gate_log[0:GPAD, :], bank[b][0:GPAD, :]).then_inc(read[b], 1)
                    elif kind == "rbc":
                        b = when_full(i, s)
                        copy(r_bc[:, :], bank[b][:, :]).then_inc(read[b], 1)
                    elif kind == "fc1":
                        b = when_full(i, s)
                        copy(lat_hi[:, s[1], :], bank[b][:, :]).then_inc(lat_hi_done.sem, 1)
                    elif kind in ("exp", "up"):
                        n = t32_order(s)
                        b = when_full(i, s)
                        if kind == "up":
                            act.wait_ge(lo_ready.sem, lo_ready.at(i, KV * 16 + n + 1 - 2))
                            nc.scalar.activation(t32[:, n % 2, :], bank[b][:, :], ACT.Relu).then_inc(relu_done.sem, 1)
                        if kind == "up" and may_split(u + 2, last):
                            split_w(i, u + 2)
                        b, v = fill(i, s)
                        act.wait_ge(read[b], v + 1)
                        dst = moe_hi[:, s[1], :] if kind == "exp" else h_hi[:, s[1], :]
                        copy(dst, t32[:, n % 2, :]).then_inc(t_hi_done.sem, 1)
                    elif kind == "down" and s[2] == DC - 1:
                        for tt in range(TT):
                            b = when_full(i, ("down", s[1], tt))
                            copy(y[:, tt, s[1] * HALF:(s[1] + 1) * HALF], bank[b][:, :]).then_inc(read[b], 1)

                    v = u if kind != "exp" else U_EXP + s[1] // 2 if s[1] % 2 else None
                    if v is not None and kind != "up" and may_split(v + 2, last):
                        split_w(i, v + 2)
                    if kind == "kv" and s[1] == 0 and s[2] + 2 < KC:
                        split_c(i, s[2] + 2)
                    if kind == "down" and s[1] == 1 and s[2] >= DC - 2 and not last:
                        split_c(i + 1, s[2] - (DC - 2))
                    if kind == "o" and s[1:] == (1, OT // 2 - 1):
                        guess_rstd(i, 1)
                    if kind == "down" and s[1:] == (0, 1) and not last:
                        guess_rstd(i, 2)
                    if kind == "down" and s[1:] == (1, DC - 1):
                        guess_rstd(i, 2 if last else 3)

            over_blocks(act, body)

        @block.gpsimd
        def _(pool):
            def lo(out_, x32, hi):
                return nc.gpsimd.tensor_tensor(out_, x32, hi.bitcast(F32), ALU.subtract)

            def split_w(i, u):
                i, u = (i, u) if u < UNITS else (i + 1, u - UNITS)
                n = unit_dram(u)[1]
                pool.wait_ge(w_hi_done.sem, w_hi_done.at(i, u + 1))
                lo(w_lo[:, u % 2, 0:n], w_st[:, u % 2, 0:n], w_hi[:, u % 2, 0:n]).then_inc(w_ready.sem, 1)

            def split_c(i, kc):
                pool.wait_ge(c_hi_done.sem, c_hi_done.at(i, kc + 1))
                lo(c_lo[:, kc % 2, :], c_st[:, kc % 2, :], c_hi[:, kc % 2, :]).then_inc(c_ready.sem, 1)

            pool.sem_inc(out_stored.sem, out_stored.credit)
            for b in range(NBANK):
                pool.sem_inc(read[b], 1)
            nc.gpsimd.memset(ident[:, :], 0.0).then_inc(zeroed, 1)
            nc.gpsimd.memset(gate_w[:, :, :].bitcast(F32), 0.0).then_inc(zeroed, 1)
            pool.wait_ge(zeroed, 2)
            nc.gpsimd.affine_select(out=ident[:, :], in_=ident[:, :], compare_op=ALU.not_equal, fill=1.0, base=0,
                                    pattern=[[-1, P]], channel_multiplier=1).then_inc(ident_ready, 1)
            pool.wait_ge(gate_hi_done, 1)
            lo(gate_w[:, :, 32:32 + EXPERTS], gate_st[:, :, :], gate_w[:, :, 0:EXPERTS]).then_inc(gate_ready, 1)
            for n in range(2):
                split_c(0, n)
                split_w(0, n)

            def body(i, last):
                for s in STEPS:
                    kind, u = s[0], unit_of(s)
                    if kind == "o" and s[1] == 0:
                        for t in range(EARLY + 3 * s[2], min(EARLY + 3 * s[2] + 3, OT)):
                            pool.wait_ge(o_hi_done.sem, o_hi_done.at(i, t + 1))
                            lo(o_part(False, t), o32[:, t, :], o_part(True, t)).then_inc(o_ready.sem, 1)
                    if kind == "up" and may_split(u + 2, last):
                        split_w(i, u + 2)

                    if kind == "kv" and s[1:] == (0, KC - 1):
                        b, v = fill(i, ("kv", 0, 0))
                        pool.wait_ge(full[b], v)
                        waited(pool)
                        nc.gpsimd.memset(v_hi[:, :, :, :, HD:P].rearrange("p c t g d -> p (c t g) d").bitcast(F32),
                                         1.0).then_inc(ones_ready.sem, 1)
                    elif kind == "score":
                        for kt in range(4):
                            k = s[1] * 16 + s[2] * 4 + kt
                            b, v = fill(i, s + (kt,))
                            pool.wait_ge(read[b], v + 1)
                            lo(p_lo[:, k % PRING].rearrange("p b s -> p (b s)"), t32[:, k % 2, :],
                               p_hi[:, k % PRING].rearrange("p b s -> p (b s)")).then_inc(lo_ready.sem, 1)
                    elif kind == "gate":
                        b, v = fill(i, ("ln2T", KC - 1))
                        pool.wait_ge(full[b], v)
                        waited(pool)
                        nc.gpsimd.memset(gate_ones[:, :], 1.0).then_inc(ones_ready.sem, 1)
                    elif kind in ("exp", "up"):
                        n = t32_order(s)
                        pool.wait_ge(t_hi_done.sem, t_hi_done.at(i, n + 1))
                        hi, dst = (moe_hi, moe_lo) if kind == "exp" else (h_hi, h_lo)
                        lo(dst[:, s[1], :], t32[:, n % 2, :], hi[:, s[1], :]).then_inc(lo_ready.sem, 1)
                    elif kind == "down" and s[1:] == (0, 2):
                        pool.wait_ge(gb_loaded.sem, gb_loaded.at(i, 2))
                        pool.wait_ge(tanh_ready, 1)
                        pool.wait_ge(xn2_ready.sem, xn2_ready.at(i, TT))
                        waited(pool)
                        nc.gpsimd.tensor_scalar(bet[:, :], bet[:, :], tg[:, 1:2], None, ALU.mult)
                        nc.gpsimd.tensor_scalar(gam[:, :], gam[:, :], tg[:, 1:2], None,
                                                ALU.mult).then_inc(pool_chain.sem, 1)
                        pool.wait_ge(pool_chain.sem, pool_chain.at(i, 1))
                    elif kind == "down" and s[1] == 0 and 3 <= s[2] < 3 + TT:
                        tt = s[2] - 3
                        op = nc.gpsimd.tensor_tensor(x2[:, tt, :], x2[:, tt, :], bet[:, :], ALU.add)
                        if tt == TT - 1:
                            op.then_inc(gb_ready.sem, 1)

                    v = u if kind != "exp" else U_EXP + s[1] // 2 if s[1] % 2 else None
                    if v is not None and kind != "up" and may_split(v + 2, last):
                        split_w(i, v + 2)
                    if kind == "kv" and s[1] == 0 and s[2] + 2 < KC:
                        split_c(i, s[2] + 2)
                    if kind == "down" and s[1] == 1 and s[2] >= DC - 2 and not last:
                        split_c(i + 1, s[2] - (DC - 2))

            over_blocks(pool, body)

        @block.vector
        def _(dve):
            v_ = nc.vector
            links = [0]

            def link(i, op):
                links[0] += 1
                op.then_inc(dve_chain.sem, 1)
                dve.wait_ge(dve_chain.sem, AHEAD_LINKS + dve_chain.at(i, links[0]) if i is not None else links[0])

            def when_full(i, job):
                b, v = fill(i, job)
                dve.wait_ge(full[b], v)
                return b

            def stats(src, tt, h):
                return v_.bn_stats(bn[:, tt, h, :], src[:, tt, h * HALF:(h + 1) * HALF])

            def mean_var(i, ki, k):
                waited(dve)
                for tt in range(TT):
                    op = v_.bn_aggr(mv[:, tt, :], bn[:, tt, :, :].rearrange("p a b -> p (a b)"))
                link(i, op)
                v_.tensor_scalar(var[:, :], mv[:, :, 1], EPS, None, ALU.add).then_inc(var_ready.sem, 1)
                dve.wait_ge(rstd_guess.sem, rstd_guess.at(ki, k))
                link(i, v_.tensor_tensor(newt[:, :], rstd0[:, :], rstd0[:, :], ALU.mult))
                link(i, v_.scalar_tensor_tensor(newt[:, :], newt[:, :], -0.5, var[:, :], ALU.mult, ALU.mult))
                link(i, v_.scalar_tensor_tensor(rstd[:, :], newt[:, :], 1.5, rstd0[:, :], ALU.add, ALU.mult))

            def layernorm(dst, src, tt):
                return v_.tensor_scalar(dst[:, tt, :], src[:, tt, :], mv[:, tt, 0:1], rstd[:, tt:tt + 1],
                                        ALU.subtract, ALU.mult)

            def lo(out_, x32, hi):
                return v_.tensor_tensor(out_, x32, hi.bitcast(F32), ALU.subtract)

            link(None, v_.memset(row_max[:, :], 0.0))
            dve.wait_ge(ident_ready, 1)
            link(None, v_.tensor_scalar(neg_mask[:, :], ident[0:GROUP, 0:GROUP], -1.0, None, ALU.mult))
            dve.wait_ge(tanh_ready, 1)
            for tt in range(TT):
                dve.wait_ge(x_loaded[tt].sem, 16)
                stats(rows, tt, 0)
                op = stats(rows, tt, 1)
            link(None, op)
            mean_var(None, 0, 0)
            for tt in range(TT):
                layernorm(rows, rows, tt).then_inc(xn_ready.sem, 1)
            for kc in range(KC):
                b = when_full("ahead", ("ln1T", kc))
                dve.wait_ge(x1_hi.sem, kc + 1)
                lo(x_lo[:, kc, :], bank[b][:, :], x_hi[:, kc, :]).then_inc(read[b], 1)
            assert links[0] == AHEAD_LINKS, links[0]

            def body(i, last):
                links[0] = 0
                for s in VECTOR_STEPS:
                    kind = s[0]
                    if kind == "kv" and s[2] == KC - 1:
                        src = s[1]
                        if src == 0:
                            when_full(i, ("kv", 0, 0))
                            v_.memset(k_hi[96:96 + GROUP].rearrange("p g b c s -> p (g b c s)").bitcast(F32), 1.0)
                        for t in range(HT):
                            b = when_full(i, ("kv", src, t))
                            dve.wait_ge(kv_hi.sem, kv_hi.at(i, src * (HT + TT) + t + 1))
                            lo(k_lo[0:96, t, :, src, :], bank[b][0:96, :].rearrange("p (b s) -> p b s", b=BPB),
                               k_hi[0:96, t, :, src, :])
                            lo(k_lo[32 * t:32 * t + 32, 3, :, src, :],
                               bank[b][96:128, :].rearrange("p (b s) -> p b s", b=BPB),
                               k_hi[32 * t:32 * t + 32, 3, :, src, :]).then_inc(read[b], 1)
                        for tt in range(TT):
                            b = when_full(i, ("kv", src, HT + tt))
                            dve.wait_ge(kv_hi.sem, kv_hi.at(i, src * (HT + TT) + HT + tt + 1))
                            lo(v_lo[:, src, tt, :, :], bank[b][:, 0:KV * HD].rearrange("p (g d) -> p g d", g=KV),
                               v_hi[:, src, tt, :, 0:HD]).then_inc(read[b], 1)
                    elif kind == "q":
                        g, t = s[1:]
                        b = when_full(i, s)
                        dve.wait_ge(q_hi_done.sem, q_hi_done.at(i, g * HT + t + 1))
                        lo(q_lo[g % 2][0:96, t, :], bank[b][0:96, :], q_hi[g % 2][0:96, t, :])
                        lo(q_lo[g % 2][32 * t:32 * t + 32, 3, :], bank[b][96:128, :],
                           q_hi[g % 2][32 * t:32 * t + 32, 3, :]).then_inc(read[b], 1)
                    elif kind == "max":
                        g, h = s[1:]
                        if h == 0 and g:
                            b, v = fill(i, ("maxT", g - 1))
                            dve.wait_ge(full[b], v)
                        for tt in range(TT):
                            b = when_full(i, s + (tt,))
                            v_.reduce_max(row_max[:, tt * GROUP + h:tt * GROUP + h + 1], bank[b][:, :],
                                          AX.X).then_inc(read[b], 1)
                    elif kind == "maxT":
                        g = s[1]
                        b = when_full(i, s)
                        v_.tensor_tensor(q_hi[g % 2][96:96 + GROUP, :, :],
                                         bank[b][0:GROUP, :].unsqueeze(1).broadcast_to([GROUP, GROUP, TOK]),
                                         neg_mask[:, :].unsqueeze(2).broadcast_to([GROUP, GROUP, TOK]),
                                         ALU.mult).then_inc(read[b], 1)
                    elif kind == "pv":
                        g, n = s[1:]
                        bt, pair = n // 2, n % 2
                        b = when_full(i, s)
                        acc = bank[b][:, :].rearrange("p (h s) -> p h s", h=2)
                        dve.wait_ge(inv_ready.sem, inv_ready.at(i, g * 4 + n + 1))
                        r = slice(32 * (n % 2), 32 * (n % 2) + 32)
                        guess, inv = inv_guess[r], neg_inv[r]
                        link(i, v_.tensor_tensor(inv, acc[96:128], guess, ALU.mult))
                        link(i, v_.scalar_tensor_tensor(inv, inv, 2.0, guess, ALU.subtract, ALU.mult))
                        o_t = o32[:, HT * g:HT * g + HT, :].rearrange("p t (b s) -> p t b s", b=BPB)
                        for j in range(HT):
                            r = slice(32 * j, 32 * j + 32)
                            if pair == 0:
                                op = v_.scalar_tensor_tensor(o_t[r, 0:2, bt, :], acc[r], -1.0, inv,
                                                             ALU.mult, ALU.mult)
                            else:
                                v_.scalar_tensor_tensor(o_t[r, 2, bt, :], acc[r, 0, :], -1.0, inv[:, 0, :],
                                                        ALU.mult, ALU.mult)
                                op = v_.scalar_tensor_tensor(o_t[96:128, j, bt, :], acc[r, 1, :], -1.0,
                                                             inv[:, 1, :], ALU.mult, ALU.mult)
                        op.then_inc(read[b], 1)
                        if (g, n) == (KV - 1, 0):
                            for t in range(EARLY):
                                dve.wait_ge(o_hi_done.sem, o_hi_done.at(i, t + 1))
                                lo(o_part(False, t), o32[:, t, :], o_part(True, t)).then_inc(oe_ready.sem, 1)
                    elif kind == "o" and s[2] == OT // 2 - 1:
                        half = s[1]
                        dve.wait_ge(xres_loaded.sem, xres_loaded.at(i, 1))
                        for tt in range(TT):
                            b = when_full(i, ("o", half, tt))
                            xs = x2[:, tt, half * HALF:(half + 1) * HALF]
                            op = v_.scalar_tensor_tensor(xs, bank[b][:, :], tg[:, 0:1], xs, ALU.mult, ALU.add)
                            op.then_inc(read[b], 1)
                            b, v = fill(i, ("o", half, tt))
                            dve.wait_ge(read[b], v + 1)
                            op = stats(x2, tt, half)
                        if half == 1:
                            link(i, op)
                            dve.wait_ge(o_ready.sem, o_ready.at(i, OT - EARLY))
                            mean_var(i, i, 1)
                            for tt in range(TT):
                                op = layernorm(rows, x2, tt)
                                op.then_inc(xn2_ready.sem, 1)
                    elif kind == "ln2T":
                        b = when_full(i, s)
                        dve.wait_ge(x2_hi.sem, x2_hi.at(i, s[1] + 1))
                        lo(x_lo[:, s[1], :], bank[b][:, :], x_hi[:, s[1], :]).then_inc(read[b], 1)
                    elif kind == "gateT":
                        b = when_full(i, s)
                        t4 = bank[b][:, :].rearrange("p (t e) -> p t e", t=TT)
                        link(i, v_.tensor_copy(logits[:, :, :], t4[:, :, 0:EXPERTS]))
                        v_.tensor_tensor(logits[:, :, :], logits[:, :, :], t4[:, :, 32:32 + EXPERTS],
                                         ALU.add).then_inc(read[b], 1)
                        b, v = fill(i, s)
                        dve.wait_ge(read[b], v + 1)
                        waited(dve)
                        for tt in range(TT):
                            op = v_.max(top8[:, tt, :], logits[:, tt, :])
                        link(i, op)
                        link(i, v_.tensor_tensor(r_sum[:, :], top8[:, :, 0], top8[:, :, 1], ALU.add))
                        for tt in range(TT):
                            op = v_.tensor_scalar(r_diag[:, tt * P:(tt + 1) * P], ident[:, :], r_sum[:, tt:tt + 1],
                                                  None, ALU.mult)
                        op.then_inc(diag_ready.sem, 1)
                    elif kind == "fc1":
                        b = when_full(i, s)
                        dve.wait_ge(lat_hi_done.sem, lat_hi_done.at(i, s[1] + 1))
                        lo(lat_lo[:, s[1], :], bank[b][:, :], lat_hi[:, s[1], :]).then_inc(read[b], 1)
                    elif kind == "exp":
                        n = t32_order(s)
                        b, v = fill(i, ("rbc",))
                        dve.wait_ge(read[b], v + 1)
                        b = when_full(i, s)
                        dve.wait_ge(lo_ready.sem, lo_ready.at(i, KV * 16 + n + 1 - 2))
                        v_.tensor_tensor(t32[:, n % 2, :], bank[b][:, :], r_bc[:, :], ALU.mult).then_inc(read[b], 1)
                    elif kind == "up":
                        n = t32_order(s)
                        b = when_full(i, s)
                        dve.wait_ge(relu_done.sem, relu_done.at(i, s[1] + 1))
                        v_.scalar_tensor_tensor(t32[:, n % 2, :], bank[b][:, :], 0.0, t32[:, n % 2, :],
                                                ALU.max, ALU.mult).then_inc(read[b], 1)
                    elif kind == "down" and s[1:] == (0, 0) and not last:
                        for tt in range(TT):
                            dve.wait_ge(x_loaded[tt].sem, x_loaded[tt].at(i + 1, 1))
                            stats(rows, tt, 0)
                            op = stats(rows, tt, 1)
                        link(i, op)
                        mean_var(i, i, 2)
                        for tt in range(TT):
                            layernorm(rows, rows, tt).then_inc(xn_ready.sem, 1)
                    elif kind == "ln1T" and not last:
                        b = when_full(i, s)
                        dve.wait_ge(x1_hi.sem, x1_hi.at(i + 1, s[1] + 1))
                        lo(x_lo[:, s[1], :], bank[b][:, :], x_hi[:, s[1], :]).then_inc(read[b], 1)
                    elif kind == "down" and s[2] == DC - 1:
                        for tt in range(TT):
                            b, v = fill(i, ("down", s[1], tt))
                            dve.wait_ge(read[b], v + 1)
                            op = stats(y, tt, s[1])
                        if s[1] == 1:
                            link(i, op)
                            mean_var(i, i, 2 if last else 3)
                            dve.wait_ge(gb_ready.sem, gb_ready.at(i, 1))
                            for tt in range(TT):
                                op = v_.scalar_tensor_tensor(y[:, tt, :], y[:, tt, :], mv[:, tt, 0:1], gam[:, :],
                                                             ALU.subtract, ALU.mult)
                            link(i, op)
                            for tt in range(TT):
                                v_.scalar_tensor_tensor(y[:, tt, :], y[:, tt, :], rstd[:, tt:tt + 1], x2[:, tt, :],
                                                        ALU.mult, ALU.add).then_inc(y_ready.sem, 1)
                assert last or links[0] == DVE_LINKS, links[0]

            over_blocks(dve, body)

        @block.tensor
        def _(pe):
            mm = nc.tensor.matmul

            def split_product(out_, w, wl, m, ml, first, final):
                mm(out_, w, m, start=first, stop=False)
                mm(out_, w, ml, start=False, stop=False)
                return mm(out_, wl, m, start=False, stop=final)

            def when_free(i, job):
                b, v = fill(i, job)
                pe.wait_ge(read[b], v)
                return b

            def when_read(i, job):
                b, v = fill(i, job)
                pe.wait_ge(read[b], v + 1)

            def transpose_rows(i, job, kc):
                b = when_free(i, job)
                for tt in range(TT):
                    op = nc.tensor.transpose(bank[b][:, tt * P:(tt + 1) * P], rows[:, tt, kc * P:(kc + 1) * P],
                                             ident[:, :])
                op.then_inc(full[b], 1)

            pe.wait_ge(ident_ready, 1)
            pe.wait_ge(xn_ready.sem, TT)
            for kc in range(KC):
                transpose_rows("ahead", ("ln1T", kc), kc)
            pe.wait_ge(gate_ready, 1)

            def body(i, last):
                for s in STEPS:
                    kind, u = s[0], unit_of(s)
                    if kind == "exp":
                        u = U_EXP + s[1] // 2
                    if u is not None:
                        pe.wait_ge(w_ready.sem, w_ready.at(i, u + 1))
                        wh, wl = w_hi[:, u % 2, :], w_lo[:, u % 2, :]
                    op = None
                    if kind == "kv":
                        src, kc = s[1:]
                        if src == 0:
                            pe.wait_ge(c_ready.sem, c_ready.at(i, kc + 1))
                            ah, al = c_hi[:, kc % 2, :], c_lo[:, kc % 2, :]
                        else:
                            ah, al = x_hi[:, kc, :], x_lo[:, kc, :]
                            if kc == 0:
                                b, _ = BANK[("ln1T", KC - 1)]
                                pe.wait_ge(read[b], i * FILLS[b] + (FILLS_AHEAD[b] + 1))
                        first, final = kc == 0, kc == KC - 1
                        for t in range(HT):
                            job = ("kv", src, t)
                            b = when_free(i, job) if first else fill(i, job)[0]
                            op = split_product(bank[b][:, :], wh[:, t * P:(t + 1) * P], wl[:, t * P:(t + 1) * P],
                                               ah, al, first, final)
                            if final:
                                op.then_inc(full[b], 1)
                        for tt in range(TT):
                            job = ("kv", src, HT + tt)
                            b = when_free(i, job) if first else fill(i, job)[0]
                            tok = slice(tt * P, (tt + 1) * P)
                            op = split_product(bank[b][:, 0:KV * HD], ah[:, tok], al[:, tok],
                                               wh[:, HT * P:KVW], wl[:, HT * P:KVW], first, final)
                            if final:
                                op.then_inc(full[b], 1)
                    elif kind in ("q", "fc1", "up"):
                        if kind == "fc1" and s[1] == 0:
                            when_read(i, ("ln2T", KC - 1))
                        b = when_free(i, s)
                        for kc in range(KC):
                            c = slice(kc * P, (kc + 1) * P)
                            op = split_product(bank[b][:, :], wh[:, c], wl[:, c], x_hi[:, kc, :], x_lo[:, kc, :],
                                               kc == 0, kc == KC - 1)
                        op.then_inc(full[b], 1)
                    elif kind == "exp":
                        if s[1] == 0:
                            when_read(i, ("fc1", LT - 1))
                        b = when_free(i, s)
                        for kc in range(LT):
                            at = ((s[1] % 2) * LT + kc) * P
                            op = split_product(bank[b][:, :], wh[:, at:at + P], wl[:, at:at + P],
                                               lat_hi[:, kc, :], lat_lo[:, kc, :], kc == 0, kc == LT - 1)
                        op.then_inc(full[b], 1)
                    elif kind == "max":
                        g, h = s[1:]
                        when_read(i, ("q", g, min(h, HT - 1)))
                        if s[1:] == (0, 0):
                            when_read(i, ("kv", 1, HT + TT - 1))
                        for tt in range(TT):
                            b = when_free(i, s + (tt,))
                            mm(bank[b][:, :], q_hi[g % 2][0:HD, h, tt * P:(tt + 1) * P],
                               k_hi[0:HD, g, tt // 2, :, :].rearrange("p c s -> p (c s)"),
                               start=True, stop=True).then_inc(full[b], 1)
                    elif kind == "maxT":
                        when_read(i, ("max", s[1], TT - 1, GROUP - 1))
                        b = when_free(i, s)
                        for tt in range(TT):
                            op = nc.tensor.transpose(bank[b][:, tt * P:(tt + 1) * P],
                                                     row_max[:, tt * GROUP:tt * GROUP + P], ident[:, :])
                        op.then_inc(full[b], 1)
                    elif kind == "score":
                        g, n = s[1:]
                        bt, pair = n // 2, n % 2
                        if n == 0:
                            pe.wait_ge(ones_ready.sem, ones_ready.at(i, 1))
                            when_read(i, ("maxT", g))
                        heads, tok = slice(2 * pair, 2 * pair + 2), slice(bt * SEQ, (bt + 1) * SEQ)
                        A = HD + GROUP
                        for kt in range(4):
                            b = when_free(i, s + (kt,))
                            keys = slice(kt % 2 * P, (kt % 2 + 1) * P)
                            mm(bank[b][:, :], k_hi[0:A, g, bt, kt // 2, keys], q_hi[g % 2][0:A, heads, tok],
                               start=True, stop=False)
                            mm(bank[b][:, :], k_hi[0:HD, g, bt, kt // 2, keys], q_lo[g % 2][0:HD, heads, tok],
                               start=False, stop=False)
                            mm(bank[b][:, :], k_lo[0:HD, g, bt, kt // 2, keys], q_hi[g % 2][0:HD, heads, tok],
                               start=False, stop=True).then_inc(full[b], 1)
                    elif kind == "pv":
                        g, n = s[1:]
                        b = when_free(i, s)
                        for kt in range(4):
                            k = g * 16 + n * 4 + kt
                            pe.wait_ge(lo_ready.sem, lo_ready.at(i, k + 1))
                            tt = n // 2 * 2 + kt % 2
                            ph, pl = (p[:, k % PRING].rearrange("p b s -> p (b s)") for p in (p_hi, p_lo))
                            mm(bank[b][:, :], v_hi[:, kt // 2, tt, g, :], ph, start=kt == 0, stop=False)
                            mm(bank[b][0:HD, :], v_lo[:, kt // 2, tt, g, :], ph, start=False, stop=False)
                            op = mm(bank[b][:, :], v_hi[:, kt // 2, tt, g, :], pl, start=False, stop=kt == 3)
                            if kt < 3:
                                op.then_inc(p_used.sem, 1)
                        op.then_inc(full[b], 1)
                    elif kind in ("o", "down"):
                        half, c = s[1:]
                        n_chunks = OT if kind == "o" else LT + UT
                        parts = []
                        for t in (2 * c, 2 * c + 1):
                            if kind == "o":
                                parts.append((o_part(True, t), o_part(False, t)))
                            elif t < LT:
                                parts.append((moe_hi[:, t, :], moe_lo[:, t, :]))
                            else:
                                parts.append((h_hi[:, t - LT, :], h_lo[:, t - LT, :]))
                        if half == 0:
                            if kind == "down":
                                n = t32_order(("exp", t) if t < LT else ("up", t - LT))
                                pe.wait_ge(lo_ready.sem, lo_ready.at(i, KV * 16 + n + 1))
                            elif t < EARLY:
                                pe.wait_ge(oe_ready.sem, oe_ready.at(i, t + 1))
                            else:
                                pe.wait_ge(o_ready.sem, o_ready.at(i, t - EARLY + 1))
                        for tt in range(TT):
                            job, tok = (kind, half, tt), slice(tt * P, (tt + 1) * P)
                            b = when_free(i, job) if c == 0 else fill(i, job)[0]
                            for e, (ah, al) in enumerate(parts):
                                n = slice(e * HALF, (e + 1) * HALF)
                                first, final = 2 * c + e == 0, 2 * c + e == n_chunks - 1
                                op = split_product(bank[b][:, :], ah[:, tok], al[:, tok], wh[:, n], wl[:, n],
                                                   first, final)
                            if final:
                                op.then_inc(full[b], 1)
                    elif kind == "ln2T":
                        if s[1] == 0:
                            pe.wait_ge(xn2_ready.sem, xn2_ready.at(i, TT))
                        transpose_rows(i, s, s[1])
                    elif kind == "ln1T" and not last:
                        if s[1] == 0:
                            pe.wait_ge(xn_ready.sem, xn_ready.at(i + 1, TT))
                        transpose_rows(i, s, s[1])
                    elif kind == "gate":
                        b = when_free(i, s)
                        for kc in range(KC):
                            when_read(i, ("ln2T", kc))
                            mm(bank[b][0:GPAD, :], gate_w[:, kc, :], x_hi[:, kc, :], start=kc == 0, stop=False)
                            op = mm(bank[b][0:GPAD, :], gate_w[:, kc, :], x_lo[:, kc, :], start=False,
                                    stop=kc == KC - 1)
                        op.then_inc(full[b], 1)
                    elif kind == "gateT":
                        when_read(i, ("gate",))
                        b = when_free(i, s)
                        for tt in range(TT):
                            op = nc.tensor.transpose(bank[b][:, tt * P:tt * P + GPAD],
                                                     gate_log[0:GPAD, tt * P:(tt + 1) * P], ident[0:GPAD, 0:GPAD])
                        op.then_inc(full[b], 1)
                    elif kind == "rbc":
                        pe.wait_ge(ones_ready.sem, ones_ready.at(i, 2))
                        pe.wait_ge(diag_ready.sem, diag_ready.at(i, 1))
                        b = when_free(i, s)
                        mm(bank[b][:, :], gate_ones[:, :], r_diag[:, :], start=True, stop=True).then_inc(full[b], 1)
                    if u in COUNTED:
                        op.then_inc(w_used.sem, 1)

            over_blocks(pe, body)


def kernel(x, ctx_4096, g_xattn, g_ffn, L0_xattn_Wq, L0_xattn_Wk, L0_xattn_Wv, L0_xattn_Wo, L0_ffn_gate_w,
           L0_ffn_up_w, L0_ffn_down_w, L0_ffn_fc1_w, L0_ffn_fc2_w, L0_ffn_expert_w, L0_ffn_ln_gamma, L0_ffn_ln_beta):
    import numpy as np
    import concourse.bacc as bacc
    from concourse.bass_utils import run_bass_kernel_spmd

    x, ctx, Wq, Wk, Wv, Wo, gate, up, down, fc1, fc2, expert, gamma, beta = (np.asarray(a) for a in (
        x, ctx_4096, L0_xattn_Wq, L0_xattn_Wk, L0_xattn_Wv, L0_xattn_Wo, L0_ffn_gate_w, L0_ffn_up_w, L0_ffn_down_w,
        L0_ffn_fc1_w, L0_ffn_fc2_w, L0_ffn_expert_w, L0_ffn_ln_gamma, L0_ffn_ln_beta))
    group = np.concatenate([np.r_[t * HD:(t + 1) * HD, 3 * HD + 32 * t:3 * HD + 32 * t + 32] for t in range(HT)])
    order = np.concatenate([g * GROUP * HD + group for g in range(KV)])

    def stationary(w, chunks, tiles=1):
        n = w.shape[1] // (P * tiles)
        return w.reshape(chunks, P, n, tiles, P).transpose(2, 1, 3, 0, 4).reshape(n, P, tiles * chunks * P)

    def moving(w):
        n = w.shape[0] // (2 * P)
        return w.reshape(n, 2, P, 2, HALF).transpose(3, 0, 2, 1, 4).reshape(2 * n, P, DIM)

    arrays = {
        "x": x.reshape(-1, DIM),
        "ctxT": ctx.reshape(BLOCKS, TOK, KC, P).transpose(0, 2, 3, 1),
        "g_x": g_xattn, "g_f": g_ffn,
        "w_kv": np.concatenate([Wk.T[:, group], Wv.T], axis=1).reshape(KC, P, KVW),
        "w_q": stationary(Wq.T[:, order], KC),
        "w_o": moving(Wo.T[order]),
        "w_fc1": stationary(fc1, KC),
        "w_exp": stationary(expert, LT, 2),
        "w_up": stationary(up, KC),
        "w_down": moving(np.concatenate([fc2, down])),
        "w_gate": gate.reshape(KC, P, EXPERTS).transpose(1, 0, 2),
        "gamma": gamma, "beta": beta,
    }
    arrays = {f"in_{k}": np.ascontiguousarray(np.asarray(a)) for k, a in arrays.items()}
    nc = bacc.Bacc("TRN2", target_bir_lowering=False, num_devices=1)
    args = [nc.dram_tensor(k, a.shape, F32, kind="ExternalInput").ap() for k, a in arrays.items()]
    args.append(nc.dram_tensor("out", (BATCH * SEQ, DIM), F32, kind="ExternalOutput").ap())
    layer_kernel(nc, *args)
    r = run_bass_kernel_spmd(nc, [arrays], core_ids=[0])
    return r.results[0]["out"].reshape(BATCH, SEQ, DIM)
```

```python
from contextlib import ExitStack

import concourse.bass as bass
from concourse import mybir
from concourse.alu_op_type import AluOpType as ALU

F32 = mybir.dt.float32
F32R = mybir.dt.float32r
ACT = mybir.ActivationFunctionType
AX = mybir.AxisListType

BATCH, SEQ, DIM = 8, 256, 1024
KV, GROUP, HD = 4, 4, 96
INT, LAT, EXPERTS = 2048, 512, 8
EPS = 1e-5
SCALE = float(HD) ** -0.5
P = 128
TOK = 512
BLOCKS = BATCH * SEQ // TOK
BPB = TOK // SEQ
TT = TOK // P
KC = DIM // P
HT = 3
OT = KV * HT
UT = INT // P
LT = LAT // P
HALF = DIM // 2
KVW = HT * P + KV * HD
GPAD = 66
DC = (LT + UT) // 2
MXW = TT * GROUP + P - GROUP

U_CTX = 0
U_Q00 = U_CTX + KC
U_X = U_Q00 + 1
U_Q = U_X + KC - 1
U_O = U_Q + KV * HT
U_FC1 = U_O + 2 * (OT // 2)
U_UP0 = U_FC1 + LT
U_EXP = U_UP0 + 2
U_UP2 = U_EXP + LT // 2
U_DOWN = U_UP2 + UT - 2
UNITS = U_DOWN + 2 * DC
assert UNITS % 2 == 0
UNIT_UP = [U_UP0, U_UP0 + 1] + [U_UP2 + j for j in range(UT - 2)]

U_LO_DVE = U_FC1 - 1
EARLY = 4
PRING = 6
NBANK = 8


def steps_main():
    s = [("kv", 0, kc) for kc in range(KC)] + [("q", 0, 0)] + [("kv", 1, kc) for kc in range(KC)]
    s += [("q", 0, 1), ("max", 0, 0), ("max", 0, 1), ("q", 0, 2), ("max", 0, 2), ("max", 0, 3), ("q", 1, 0),
          ("maxT", 0), ("q", 1, 1)]
    for g in range(KV):
        n = g + 1
        if g == 0:
            order = [("max", n, 0), ("score", g, 0), ("q", n, 2), ("max", n, 1), ("score", g, 1), ("pv", g, 0),
                     ("max", n, 2), ("score", g, 2), ("pv", g, 1)]
        elif n < KV:
            order = [("max", n, 0), ("score", g, 0), ("q", n, 1), ("pv", g, 0), ("max", n, 1), ("score", g, 1),
                     ("q", n, 2), ("max", n, 2), ("score", g, 2), ("pv", g, 1)]
        else:
            order = [("score", g, 0), ("score", g, 1), ("pv", g, 0), ("score", g, 2), ("pv", g, 1)]
        order += [("max", n, 3), ("score", g, 3), ("pv", g, 2), ("q", n + 1, 0), ("maxT", n), ("pv", g, 3)]
        s += [x for x in order if x[1] < KV]
    s += [("o", h, c) for h in range(2) for c in range(OT // 2)]
    a = s.index(("pv", KV - 1, 3))
    s[a], s[a + 1] = s[a + 1], s[a]
    s += [("ln2T", kc) for kc in range(KC)]
    s += [("gate",), ("fc1", 0), ("fc1", 1), ("gateT",), ("fc1", 2), ("rbc",), ("fc1", 3), ("up", 0), ("up", 1)]
    s += [("exp", j) for j in range(LT)] + [("up", j) for j in range(2, UT)]
    for c in range(DC):
        s += [("down", 0, c)]
        if 2 <= c < KC + 2:
            s += [("ln1T", c - 2)]
    s += [("down", 1, c) for c in range(DC)]
    return s


STEPS = steps_main()


def riders():
    r = {("q", 0, 2): [(h, tt, 4 * h + tt) for h in (0, 1) for tt in range(TT)],
         ("q", 1, 0): [(2, tt, 1 + tt) for tt in range(TT)] + [(3, tt, 4 + tt) for tt in range(TT)]}
    r = {s: [(("max", 0, h, tt), at) for h, tt, at in v] for s, v in r.items()}
    r["q", 1, 1] = [(("maxT", 0), 2)]
    for g in range(KV - 1):
        for n in range(4):
            r["score", g, n] = [(("max", g + 1, n, tt), min(tt + (n in (0, 2)), 3)) for tt in range(TT)]
    return r


RIDERS = riders()


def bank_plan():
    jobs = []
    for s in STEPS:
        if s[0] == "kv" and s[2] == 0:
            jobs += [("kv", s[1], t) for t in range(HT + TT)]
        elif s[0] == "max":
            jobs += [("max", s[1], s[2], tt) for tt in range(TT)]
        elif s[0] == "score":
            jobs += [("score", s[1], s[2], kt) for kt in range(4)]
        elif s[0] == "o" and s[2] == 0:
            jobs += [("o", s[1], tt) for tt in range(TT)]
        elif s[0] in ("q", "maxT", "pv", "ln2T", "gate", "gateT", "rbc", "fc1", "exp", "up", "ln1T"):
            jobs += [s]
        elif s[0] == "down" and s[2] == 0:
            jobs += [("down", s[1], tt) for tt in range(TT)]
    fixed = {("gate",): 0, ("gateT",): 3, ("rbc",): 5, ("q", 0, 2): 6, ("q", 1, 1): 6, ("pv", KV - 2, 3): 5}
    fixed.update({("fc1", j): b for j, b in enumerate((1, 2, 4, 6))})
    plan, fills, turn = {}, [0] * NBANK, {}
    for j in jobs:
        kind = j[0]
        if j in fixed:
            b = fixed[j]
        elif kind == "kv":
            b = (0, 1, 2, 3, 4, 6, 7)[j[2]]
        elif kind in ("o", "down"):
            b = 4 * j[1] + j[2]
        elif kind == "ln1T":
            b = 4 + j[1] % 4
        elif kind in ("ln2T", "up"):
            b = j[1] % NBANK
        elif kind == "exp":
            b = 2 + j[1]
        elif kind == "q":
            b = 5
        else:
            kind = "max" if kind == "maxT" else kind
            lane = {"score": (0, 1, 2) if j[1] < KV - 1 else (0, 1, 2, 3, 4), "max": (3, 4), "pv": (6, 7)}[kind]
            turn[kind] = turn.get(kind, -1) + 1
            b = lane[turn[kind] % len(lane)]
        fills[b] += 1
        plan[j] = (b, fills[b])
    return plan, fills


def t32_order(s):
    return s[1] if s[0] == "up" and s[1] < 2 else 2 + s[1] if s[0] == "exp" else LT + s[1]


def vector_steps():
    s = list(STEPS)
    for k in range(1, len(s)):
        before = s[k - 1]
        if s[k][0] == "max" and (before[0] == "pv" or before in (("q", 1, 1), ("q", 2, 2), ("q", 3, 2))):
            s[k - 1], s[k] = s[k], s[k - 1]
    s.remove(("pv", KV - 1, 3))
    s.insert(s.index(("o", 0, 1)) + 1, ("pv", KV - 1, 3))
    for n in range(1, KV):
        s.remove(("maxT", n))
        s.insert(s.index(("q", n + 1, 0) if n + 1 < KV else ("pv", n - 1, 2)), ("maxT", n))
    return s


LO_DVE = [k for k in range(KV * 16) if k in (1, 3, 5, 7) or k - (KV - 1) * 16 in (3, 7, 15)]
LO_POOL = [k for k in range(KV * 16 + LT + UT) if k not in LO_DVE]

VECTOR_STEPS = vector_steps()
BANK, FILLS = bank_plan()
MEAN_LINKS = 4
AHEAD_LINKS = 2 + 2 * (1 + MEAN_LINKS)
DVE_LINKS = 2 * KV * 4 + 4 * (1 + MEAN_LINKS) + TT + 2 + 3
FILLS_AHEAD = [1] * NBANK
assert NBANK == KC


def fill(block, job):
    b, k = BANK[job]
    if isinstance(block, str):
        return job[1], 1
    if isinstance(block, int) and block == BLOCKS - 1 and job[:2] == ("down", 1):
        k -= KC // 4
    return b, block * FILLS[b] + (FILLS_AHEAD[b] + k)


def unit_of(s):
    if s[0] == "kv":
        return (U_CTX, U_X)[s[1]] + s[2]
    if s[0] == "q":
        return U_Q + s[1] * HT + s[2] if s[1:] != (0, 0) else U_Q00
    if s[0] == "o":
        return U_O + s[1] * (OT // 2) + s[2]
    if s[0] == "fc1":
        return U_FC1 + s[1]
    if s[0] == "exp" and s[1] % 2 == 0:
        return U_EXP + s[1] // 2
    if s[0] == "up":
        return UNIT_UP[s[1]]
    if s[0] == "down":
        return U_DOWN + s[1] * DC + s[2]
    return None


def unit_ends():
    ends = {}
    for s in STEPS:
        u = unit_of(s)
        if s[0] in ("q", "fc1", "up"):
            ends[u] = s
        elif s[0] == "exp" and s[1] % 2:
            ends[U_EXP + s[1] // 2] = s
        elif s[0] == "kv" and s[2] == KC - 1:
            ends[u] = ("kv", s[1], HT + TT - 1)
        elif s[0] == "o" and s[2] == OT // 2 - 1:
            ends[u] = ("o", s[1], TT - 1)
        elif s[0] == "down" and s[2] == DC - 1:
            ends[u] = ("down", s[1], TT - 1)
    return ends


def split_plan():
    plan = {}
    for k, s in enumerate(STEPS):
        u = U_EXP + s[1] // 2 if s[0] == "exp" and s[1] % 2 else None if s[0] == "exp" else unit_of(s)
        if u is None or s[0] == "up":
            continue
        if s[0] == "q":
            follows = next(x for x in STEPS[k + 1:] if x[0] not in ("max", "maxT"))
            s = follows if follows[0] == "score" else s
        plan.setdefault(s, []).append(u + 2)
    return plan


SPLITS = split_plan()
ENDS = unit_ends()
COUNTED = [u for u in range(UNITS) if u not in ENDS]


class Count:

    def __init__(self, sem, per, credit=0, step=1):
        self.sem, self.per, self.credit, self.step = sem, per, credit, step

    def at(self, block, k):
        return block * (self.per * self.step) + (self.credit + k * self.step)


def layer_kernel(nc, x, ctxT, g_x, g_f, w_kv, w_q, w_o, w_fc1, w_exp, w_up, w_down, w_gate, gamma, beta, out):
    ctx = ExitStack()
    with ctx:
        sem = lambda name: ctx.enter_context(nc.semaphore(name))

        base = (nc.sbuf_base + 31) // 32 * 32
        top = [base]

        def region(size):
            at = top[0]
            top[0] += (size + 31) // 32 * 32
            return at

        def place(name, shape, dtype, at):
            return nc.alloc_sbuf_tensor_at(name, shape, dtype, offset=at)

        K4 = 4096
        r_x = region(8 * K4)
        r_kv = region(15 * K4)
        r_p = region(6 * K4)
        r_t32 = region(K4)
        r_o32 = region(6 * K4)
        r_qa = region(4 * K4)
        r_qb = region(4 * K4)
        r_ws = region(2 * K4)
        r_wh = region(2 * K4)
        r_wl = region(2 * K4)

        x_hi = place("x_hi", [P, KC, TOK], F32R, r_x)
        x_lo = place("x_lo", [P, KC, TOK], F32R, r_x + 4 * K4)
        k_hi = place("k_hi", [P, KV, BPB, 2, SEQ], F32R, r_kv)
        k_lo = place("k_lo", [P, KV, BPB, 2, SEQ], F32R, r_kv + 4 * K4)
        v_hi = place("v_hi", [P, 2, TT, KV, P], F32R, r_kv + 8 * K4)
        v_lo = place("v_lo", [P, 2, TT, KV, HD], F32R, r_kv + 12 * K4)
        o_hi = place("o_hi", [P, OT - EARLY, TOK], F32R, r_kv)
        o_lo = place("o_lo", [P, OT - EARLY, TOK], F32R, r_kv + 4 * K4)
        oe_hi = place("oe_hi", [P, EARLY, TOK], F32R, r_qb)
        oe_lo = place("oe_lo", [P, EARLY, TOK], F32R, r_qb + 2 * K4)
        h_hi = place("h_hi", [P, UT, TOK], F32R, r_kv)
        h_lo = place("h_lo", [P, UT, TOK], F32R, r_kv + 8 * K4)
        p_hi = place("p_hi", [P, PRING, 2, SEQ], F32R, r_p)
        p_lo = place("p_lo", [P, PRING, 2, SEQ], F32R, r_p + 3 * K4)
        x2 = place("x2", [P, TT, DIM], F32, r_p + K4)
        t32 = place("t32", [P, 2, TOK], F32, r_t32)
        o32 = place("o32", [P, OT, TOK], F32, r_o32)
        rows = place("rows", [P, TT, DIM], F32, r_o32)
        gate_log = place("gate_log", [P, TOK], F32, r_o32)
        r_diag = place("r_diag", [P, TOK], F32, r_o32 + K4)
        r_bc = place("r_bc", [P, TOK], F32, r_o32 + 2 * K4)
        gate_ones = place("gate_ones", [P, P], F32, r_o32 + 3 * K4)
        gam = place("gam", [P, DIM], F32, r_o32 + 4 * K4)
        bet = place("bet", [P, DIM], F32, r_o32 + 5 * K4)
        qa_hi = place("qa_hi", [P, GROUP, TOK], F32R, r_qa)
        qa_lo = place("qa_lo", [P, GROUP, TOK], F32R, r_qa + 2 * K4)
        lat_hi = place("lat_hi", [P, LT, TOK], F32R, r_qa)
        lat_lo = place("lat_lo", [P, LT, TOK], F32R, r_qa + 2 * K4)
        y = place("y", [P, TT, DIM], F32, r_qa)
        qb_hi = place("qb_hi", [P, GROUP, TOK], F32R, r_qb)
        qb_lo = place("qb_lo", [P, GROUP, TOK], F32R, r_qb + 2 * K4)
        c_st = place("c_st", [P, 2, TOK], F32, r_qb)
        c_hi = place("c_hi", [P, 2, TOK], F32R, r_qb + K4)
        c_lo = place("c_lo", [P, 2, TOK], F32R, r_qb + 2 * K4)
        moe_hi = place("moe_hi", [P, LT, TOK], F32R, r_qb)
        moe_lo = place("moe_lo", [P, LT, TOK], F32R, r_qb + 2 * K4)
        w_st = place("w_st", [P, 2, DIM], F32, r_ws)
        w_hi = place("w_hi", [P, 2, DIM], F32R, r_wh)
        w_lo = place("w_lo", [P, 2, DIM], F32R, r_wl)
        ident = place("ident", [P, P], F32, region(4 * P))
        gate_w = place("gate_w", [P, KC, GPAD], F32R, region(4 * KC * GPAD))
        inv_guess = place("inv_guess", [64, 2, SEQ], F32, region(4 * TOK))
        neg_inv = place("neg_inv", [64, 2, SEQ], F32, region(4 * TOK))
        gate_st = place("gate_st", [P, KC, EXPERTS], F32, r_t32)
        row_max = place("row_max", [P, MXW], F32, region(4 * MXW))
        neg_mask = place("neg_mask", [GROUP, GROUP], F32, region(32))
        bn = place("bn", [P, TT, 2, 6], F32, region(192))
        mv = place("mv", [P, TT, 2], F32, region(32))
        var = place("var", [P, TT], F32, region(32))
        rstd0 = place("rstd0", [P, TT], F32, region(32))
        newt = place("newt", [P, TT], F32, region(32))
        rstd = place("rstd", [P, TT], F32, region(32))
        logits = place("logits", [P, TT, EXPERTS], F32, region(128))
        top8 = place("top8", [P, TT, EXPERTS], F32, region(128))
        r_sum = place("r_sum", [P, TT], F32, region(32))
        nmr = place("nmr", [P, TT], F32, region(32))
        tg = place("tg", [P, 2], F32, region(32))
        assert top[0] <= nc.sbuf_usable_end, top[0] - nc.sbuf_usable_end
        o_part = lambda hi, t: ((oe_hi if hi else oe_lo)[:, t, :] if t < EARLY else
                                (o_hi if hi else o_lo)[:, t - EARLY, :])
        q_hi, q_lo = [qb_hi, qa_hi], [qb_lo, qa_lo]

        bank = [ctx.enter_context(nc.psum_tensor(f"bank{b}", [P, TOK], F32)) for b in range(NBANK)]

        full = [sem(f"bank_full{b}") for b in range(NBANK)]
        read = [sem(f"bank_read{b}") for b in range(NBANK)]
        w_loaded = [Count(sem(f"w_loaded{s}"), UNITS // 2, step=16) for s in range(2)]
        w_hi_done = Count(sem("w_hi_done"), UNITS)
        w_ready = Count(sem("w_ready"), UNITS - 1)
        w_ready_dve = Count(sem("w_ready_dve"), 1)
        w_used = Count(sem("w_used"), len(COUNTED))
        c_loaded = [Count(sem(f"c_loaded{s}"), KC // 2, step=16) for s in range(2)]
        c_hi_done = Count(sem("c_hi_done"), KC)
        c_ready = Count(sem("c_ready"), KC)
        x_loaded = [Count(sem(f"x_loaded{t}"), 1, step=16) for t in range(TT)]
        xn_ready = Count(sem("xn_ready"), TT)
        xn2_ready = Count(sem("xn2_ready"), TT - 1)
        xn2_last = Count(sem("xn2_last"), 1)
        ln2_scales = Count(sem("ln2_scales"), 2)
        x1_hi = Count(sem("x1_hi"), KC)
        x2_hi = Count(sem("x2_hi"), KC)
        kv_hi = Count(sem("kv_hi"), 2 * (HT + TT))
        ones_ready = Count(sem("ones_ready"), 2)
        q_hi_done = Count(sem("q_hi_done"), KV * HT)
        p_used = Count(sem("p_used"), KV * 4 * 3)
        lo_ready = Count(sem("lo_ready"), len(LO_POOL))
        lo_ready_dve = Count(sem("lo_ready_dve"), len(LO_DVE))
        ln_done = Count(sem("ln_done"), KV * 4)
        inv_ready = Count(sem("inv_ready"), KV * 4)
        o_hi_done = Count(sem("o_hi_done"), OT)
        oe_ready = Count(sem("oe_ready"), EARLY)
        o_ready = Count(sem("o_ready"), OT - EARLY)
        xres_loaded = [Count(sem(f"xres_loaded{t}"), 1, step=16) for t in range(TT)]
        diag_ready = Count(sem("diag_ready"), 1)
        lat_hi_done = Count(sem("lat_hi_done"), LT)
        relu_done = Count(sem("relu_done"), UT)
        t_hi_done = Count(sem("t_hi_done"), LT + UT)
        gb_loaded = Count(sem("gb_loaded"), 2, step=16)
        var_ready = Count(sem("var_ready"), 4, credit=2)
        rstd_guess = Count(sem("rstd_guess"), 4, credit=2)
        lnvar_done = Count(sem("lnvar_done"), 4, credit=2)
        y_ready = Count(sem("y_ready"), TT)
        out_stored = Count(sem("out_stored"), TT, credit=1, step=16)
        small_loaded, tanh_ready, gate_hi_done = sem("small_loaded"), sem("tanh_ready"), sem("gate_hi_done")
        zeroed, ident_ready = sem("zeroed"), sem("ident_ready")
        gate_ready = sem("gate_ready")
        dve_chain = Count(sem("dve_chain"), DVE_LINKS)
        waits_ended = sem("waits_ended")

        x_rows = x.rearrange("(i t p) d -> i t p d", t=TT, p=P)
        out_rows = out.rearrange("(i t p) d -> i t p d", t=TT, p=P)
        block = ctx.enter_context(nc.Block())

        def waited(eng):
            eng.sem_inc(waits_ended, 1)

        def over_blocks(eng, body):
            with eng.Fori(0, BLOCKS - 1) as i:
                body(i, False)
            body(BLOCKS - 1, True)

        def unit_dram(u):
            if u == U_Q00:
                return w_q[0], DIM
            if u <= U_Q:
                return w_kv[u - U_CTX if u < U_Q00 else u - U_X], KVW
            if u < U_O:
                return w_q[u - U_Q], DIM
            if u < U_FC1:
                return w_o[u - U_O], DIM
            if u < U_UP0:
                return w_fc1[u - U_FC1], DIM
            if U_EXP <= u < U_UP2:
                return w_exp[u - U_EXP], DIM
            if u < U_DOWN:
                return w_up[UNIT_UP.index(u)], DIM
            return w_down[u - U_DOWN], DIM

        def unit_used(eng, i, u):
            if u in ENDS:
                b, v = fill(i, ENDS[u])
                eng.wait_ge(full[b], v)
            else:
                eng.wait_ge(w_used.sem, w_used.at(i, COUNTED.index(u) + 1))

        def lo_done(eng, i, k):
            done, tiles = (lo_ready_dve, LO_DVE) if k in LO_DVE else (lo_ready, LO_POOL)
            eng.wait_ge(done.sem, done.at(i, tiles.index(k) + 1))

        def late_tiles(c):
            return range(2 * c + 2, min(2 * c + 4, OT)) if c else ()

        def unit_split(eng, i, u):
            if u == U_LO_DVE:
                eng.wait_ge(w_ready_dve.sem, w_ready_dve.at(i, 1))
            else:
                eng.wait_ge(w_ready.sem, w_ready.at(i, u + 1 - (u > U_LO_DVE)))

        def may_split(u, last):
            return u < UNITS or not last

        @block.sync
        def _(sp):
            def load_unit(i, u, ahead=None):
                src, n = unit_dram(u)
                if ahead is None:
                    unit_split(sp, i, u - 2)
                sp.dma_start(w_st[:, u % 2, 0:n], src).then_inc(w_loaded[u % 2].sem, 16)

            def load_ctx(i, kc):
                if kc >= 2:
                    sp.wait_ge(c_ready.sem, c_ready.at(i, kc + 1 - 2))
                    waited(sp)
                sp.dma_start(c_st[:, kc % 2, :], ctxT[i, kc]).then_inc(c_loaded[kc % 2].sem, 16)

            def load_rows(i):
                for tt in range(TT):
                    sp.dma_start(rows[:, tt, :], x_rows[i, tt]).then_inc(x_loaded[tt].sem, 16)

            sp.dma_start(rows[:, 0, :], x_rows[0, 0]).then_inc(x_loaded[0].sem, 16)
            sp.dma_start(tg[:, 0:1], g_x.partition_broadcast(P)).then_inc(small_loaded, 16)
            sp.dma_start(tg[:, 1:2], g_f.partition_broadcast(P)).then_inc(small_loaded, 16)
            sp.dma_start(gate_st[:, :, :], w_gate).then_inc(small_loaded, 16)
            for tt in range(1, TT):
                sp.dma_start(rows[:, tt, :], x_rows[0, tt]).then_inc(x_loaded[tt].sem, 16)
            load_ctx(0, 0)
            load_unit(0, 0, ahead=True)
            load_ctx(0, 1)
            load_unit(0, 1, ahead=True)
            HEAD = KC
            for u in range(2, HEAD):
                load_unit(0, u)
                load_ctx(0, u)

            def store(i, tt):
                sp.wait_ge(y_ready.sem, y_ready.at(i, tt + 1))
                waited(sp)
                sp.dma_start(out_rows[i, tt], y[:, tt, :]).then_inc(out_stored.sem, 16)

            def body(i, last):
                for u in range(HEAD, UNITS):
                    load_unit(i, u)
                    if U_O + 2 <= u < U_O + 2 + TT:
                        tt = u - (U_O + 2)
                        b, v = fill(i, ("pv", KV - 1, 3))
                        sp.wait_ge(full[b], v)
                        waited(sp)
                        sp.dma_start(x2[:, tt, :], x_rows[i, tt]).then_inc(xres_loaded[tt].sem, 16)
                    if u == U_FC1 - 2:
                        sp.wait_ge(o_ready.sem, o_ready.at(i, OT - EARLY))
                        sp.dma_start(gam[:, :], gamma.partition_broadcast(P)).then_inc(gb_loaded.sem, 16)
                        sp.dma_start(bet[:, :], beta.partition_broadcast(P)).then_inc(gb_loaded.sem, 16)
                    if u == U_DOWN - 4 and not last:
                        b, v = fill(i, ("exp", LT - 1))
                        sp.wait_ge(read[b], v + 1)
                        waited(sp)
                        load_rows(i + 1)
                if not last:
                    unit_used(sp, i, UNITS - 4)
                    waited(sp)
                    for u in range(HEAD):
                        load_ctx(i + 1, u)
                        load_unit(i + 1, u)
                        if u >= HEAD - TT:
                            store(i, u - (HEAD - TT))
                else:
                    for tt in range(TT):
                        store(i, tt)
                    sp.wait_ge(out_stored.sem, out_stored.at(i, TT))

            over_blocks(sp, body)

        @block.scalar
        def _(act):
            copy = lambda o, i_: nc.scalar.activation(o, i_, ACT.Copy)

            def split_w(i, u, ahead=None):
                n = unit_dram(u % UNITS)[1]
                if ahead is None:
                    unit_used(act, i, u - 2)
                i, u = (i, u) if u < UNITS else (i + 1, u - UNITS)
                act.wait_ge(w_loaded[u % 2].sem, w_loaded[u % 2].at(i, u // 2 + 1))
                copy(w_hi[:, u % 2, 0:n], w_st[:, u % 2, 0:n]).then_inc(w_hi_done.sem, 1)

            def split_c(i, kc):
                act.wait_ge(c_loaded[kc % 2].sem, c_loaded[kc % 2].at(i, kc // 2 + 1))
                if kc >= 2:
                    unit_used(act, i, U_CTX + kc - 2)
                copy(c_hi[:, kc % 2, :], c_st[:, kc % 2, :]).then_inc(c_hi_done.sem, 1)

            def when_full(i, job):
                b, v = fill(i, job)
                act.wait_ge(full[b], v)
                return b

            def prob_used(i, k):
                if k % 4 == 3:
                    when_full(i, ("pv", k // 16, k // 4 % 4))
                else:
                    act.wait_ge(p_used.sem, p_used.at(i, k // 4 * 3 + k % 4 + 1))

            def guess_rstd(i, k, tt=slice(0, TT)):
                act.wait_ge(var_ready.sem, var_ready.at(i, k))
                nc.scalar.activation(rstd0[:, tt], var[:, tt], ACT.Ln).then_inc(lnvar_done.sem, 1)
                act.wait_ge(lnvar_done.sem, lnvar_done.at(i, k))
                nc.scalar.activation(rstd0[:, tt], rstd0[:, tt], ACT.Exp, scale=-0.5).then_inc(rstd_guess.sem, 1)

            def layernorm2(tt):
                nc.scalar.activation(rows[:, tt, :], x2[:, tt, :], ACT.Identity, bias=nmr[:, tt:tt + 1],
                                     scale=rstd[:, tt:tt + 1]).then_inc(xn2_ready.sem, 1)

            act.wait_ge(small_loaded, 48)
            nc.scalar.activation(tg[:, :], tg[:, :], ACT.Tanh).then_inc(tanh_ready, 1)
            act.preload_act_table_set("natural_log_exp_and_others")
            act.wait_ge(zeroed, 2)
            copy(gate_w[:, :, 0:EXPERTS], gate_st[:, :, :]).then_inc(gate_hi_done, 1)
            guess_rstd(0, -1, slice(0, 2))
            guess_rstd(0, 0, slice(2, 4))
            for n in range(2):
                split_c(0, n)
                split_w(0, n, ahead=True)
            for kc in range(KC):
                b = when_full("ahead", ("ln1T", kc))
                copy(x_hi[:, kc, :], bank[b][:, :]).then_inc(x1_hi.sem, 1)

            def body(i, last):
                for s in STEPS:
                    kind, u = s[0], unit_of(s)
                    if kind == "o" and s[1:] == (0, 1):
                        when_full(i, ("pv", KV - 1, 3))
                    if kind == "o" and s[1] == 0:
                        for t in late_tiles(s[2]):
                            if t == HT * (KV - 1):
                                b, v = fill(i, ("pv", KV - 1, 3))
                                act.wait_ge(read[b], v + 1)
                            copy(o_part(True, t), o32[:, t, :]).then_inc(o_hi_done.sem, 1)

                    if kind == "kv" and s[2] == KC - 1:
                        src = s[1]
                        for t in range(HT):
                            b = when_full(i, ("kv", src, t))
                            copy(k_hi[0:96, t, :, src, :], bank[b][0:96, :].rearrange("p (b s) -> p b s", b=BPB))
                            copy(k_hi[32 * t:32 * t + 32, 3, :, src, :],
                                 bank[b][96:128, :].rearrange("p (b s) -> p b s", b=BPB)).then_inc(kv_hi.sem, 1)
                        for tt in range(TT):
                            b = when_full(i, ("kv", src, HT + tt))
                            copy(v_hi[:, src, tt, :, 0:HD],
                                 bank[b][:, 0:KV * HD].rearrange("p (g d) -> p g d", g=KV)).then_inc(kv_hi.sem, 1)
                    elif kind == "q":
                        g, t = s[1:]
                        if (g, t) == (1, 0):
                            act.wait_ge(out_stored.sem, out_stored.at(i, 0))
                        b = when_full(i, s)
                        copy(q_hi[g % 2][0:96, t, :], bank[b][0:96, :])
                        copy(q_hi[g % 2][32 * t:32 * t + 32, 3, :], bank[b][96:128, :]).then_inc(q_hi_done.sem, 1)
                    elif kind == "score":
                        g, n = s[1:]
                        if (g, n) == (0, 0):
                            act.wait_ge(out_stored.sem, out_stored.at(i, 0))
                        for kt in range(4):
                            k = g * 16 + n * 4 + kt
                            b = when_full(i, s + (kt,))
                            if k >= 2:
                                lo_done(act, i, k - 2)
                            nc.scalar.activation(t32[:, k % 2, :], bank[b][:, :], ACT.Exp, scale=SCALE)
                            if k >= PRING:
                                prob_used(i, k - PRING)
                            nc.scalar.activation(p_hi[:, k % PRING].rearrange("p b s -> p (b s)"), bank[b][:, :],
                                                 ACT.Exp, scale=SCALE).then_inc(read[b], 1)
                    elif kind == "pv":
                        n = s[1] * 4 + s[2]
                        if n >= 2:
                            b, v = fill(i, ("pv", (n - 2) // 4, (n - 2) % 4))
                            act.wait_ge(read[b], v + 1)
                        b = when_full(i, s)
                        slot = inv_guess[32 * (n % 2):32 * (n % 2) + 32]
                        nc.scalar.activation(slot, bank[b][96:128, :].rearrange("p (h s) -> p h s", h=2),
                                             ACT.Ln).then_inc(ln_done.sem, 1)
                        act.wait_ge(ln_done.sem, ln_done.at(i, n + 1))
                        nc.scalar.activation(slot, slot, ACT.Exp, scale=-1.0).then_inc(inv_ready.sem, 1)
                        if s[1:] == (KV - 2, 2):
                            for t in range(EARLY):
                                copy(o_part(True, t), o32[:, t, :]).then_inc(o_hi_done.sem, 1)
                    elif kind == "ln2T":
                        b = when_full(i, s)
                        copy(x_hi[:, s[1], :], bank[b][:, :]).then_inc(x2_hi.sem, 1)
                    elif kind == "ln1T" and not last:
                        b = when_full(i, s)
                        copy(x_hi[:, s[1], :], bank[b][:, :]).then_inc(x1_hi.sem, 1)
                    elif kind == "gate":
                        b = when_full(i, s)
                        copy(gate_log[0:GPAD, :], bank[b][0:GPAD, :]).then_inc(read[b], 1)
                    elif kind == "rbc":
                        b = when_full(i, s)
                        copy(r_bc[:, :], bank[b][:, :]).then_inc(read[b], 1)
                    elif kind == "fc1":
                        b = when_full(i, s)
                        copy(lat_hi[:, s[1], :], bank[b][:, :]).then_inc(lat_hi_done.sem, 1)
                    elif kind in ("exp", "up"):
                        n = t32_order(s)
                        b = when_full(i, s)
                        if kind == "up":
                            lo_done(act, i, KV * 16 + n - 2)
                            nc.scalar.activation(t32[:, n % 2, :], bank[b][:, :], ACT.Relu).then_inc(relu_done.sem, 1)
                        if kind == "up" and may_split(u + 2, last):
                            split_w(i, u + 2)
                        b, v = fill(i, s)
                        act.wait_ge(read[b], v + 1)
                        dst = moe_hi[:, s[1], :] if kind == "exp" else h_hi[:, s[1], :]
                        copy(dst, t32[:, n % 2, :]).then_inc(t_hi_done.sem, 1)
                    elif kind == "down" and s[2] == DC - 1:
                        for tt in range(TT):
                            b = when_full(i, ("down", s[1], tt))
                            copy(y[:, tt, s[1] * HALF:(s[1] + 1) * HALF], bank[b][:, :]).then_inc(read[b], 1)
                            if s[1] == 1 and not last and tt == TT - 2:
                                split_w(i, u + 2)
                            if s[1] == 1 and last:
                                guess_rstd(i, 3 + tt, slice(tt, tt + 1))

                    if kind == "o" and s[1:] == (1, OT // 2 - 2):
                        guess_rstd(i, 1, slice(0, 2))
                        act.wait_ge(ln2_scales.sem, ln2_scales.at(i, 1))
                        act.wait_ge(o_ready.sem, o_ready.at(i, OT - EARLY))
                        for tt in range(2):
                            layernorm2(tt)

                    if kind == "o" and s[1:] == (1, OT // 2 - 1):
                        guess_rstd(i, 2, slice(2, 4))
                        act.wait_ge(ln2_scales.sem, ln2_scales.at(i, 2))
                        layernorm2(2)

                    for v in SPLITS.get(s, ()):
                        if may_split(v, last) and v != UNITS + 1:
                            split_w(i, v)
                    if kind == "kv" and s[1] == 0 and s[2] + 2 < KC:
                        split_c(i, s[2] + 2)
                    if kind == "down" and s[1] == 1 and s[2] >= DC - 2 and not last:
                        split_c(i + 1, s[2] - (DC - 2))
                    if kind == "down" and s[1:] == (0, 1) and not last:
                        guess_rstd(i, 3)
                    if kind == "down" and s[1:] == (1, DC - 1) and not last:
                        guess_rstd(i, 4)

            over_blocks(act, body)

        @block.gpsimd
        def _(pool):
            def lo(out_, x32, hi):
                return nc.gpsimd.tensor_tensor(out_, x32, hi.bitcast(F32), ALU.subtract)

            def split_w(i, u):
                if u == U_LO_DVE:
                    return
                i, u = (i, u) if u < UNITS else (i + 1, u - UNITS)
                n = unit_dram(u)[1]
                pool.wait_ge(w_hi_done.sem, w_hi_done.at(i, u + 1))
                lo(w_lo[:, u % 2, 0:n], w_st[:, u % 2, 0:n], w_hi[:, u % 2, 0:n]).then_inc(w_ready.sem, 1)

            def split_c(i, kc):
                pool.wait_ge(c_hi_done.sem, c_hi_done.at(i, kc + 1))
                lo(c_lo[:, kc % 2, :], c_st[:, kc % 2, :], c_hi[:, kc % 2, :]).then_inc(c_ready.sem, 1)

            pool.sem_inc(out_stored.sem, out_stored.credit)
            for b in range(NBANK):
                pool.sem_inc(read[b], 1)
            nc.gpsimd.memset(ident[:, :], 0.0).then_inc(zeroed, 1)
            nc.gpsimd.memset(gate_w[:, :, :].bitcast(F32), 0.0).then_inc(zeroed, 1)
            pool.wait_ge(zeroed, 2)
            nc.gpsimd.affine_select(out=ident[:, :], in_=ident[:, :], compare_op=ALU.not_equal, fill=1.0, base=0,
                                    pattern=[[-1, P]], channel_multiplier=1).then_inc(ident_ready, 1)
            pool.wait_ge(gate_hi_done, 1)
            lo(gate_w[:, :, 32:32 + EXPERTS], gate_st[:, :, :], gate_w[:, :, 0:EXPERTS]).then_inc(gate_ready, 1)
            for n in range(2):
                split_c(0, n)
                split_w(0, n)

            def body(i, last):
                for s in STEPS:
                    kind, u = s[0], unit_of(s)
                    if kind == "up" and may_split(u + 2, last):
                        split_w(i, u + 2)

                    if kind == "kv" and s[1:] == (0, KC - 1):
                        b, v = fill(i, ("kv", 0, 0))
                        pool.wait_ge(full[b], v)
                        waited(pool)
                        nc.gpsimd.memset(v_hi[:, :, :, :, HD:P].rearrange("p c t g d -> p (c t g) d").bitcast(F32),
                                         1.0).then_inc(ones_ready.sem, 1)
                    elif kind == "score":
                        for kt in range(4):
                            k = s[1] * 16 + s[2] * 4 + kt
                            if k in LO_DVE:
                                continue
                            b, v = fill(i, s + (kt,))
                            pool.wait_ge(read[b], v + 1)
                            lo(p_lo[:, k % PRING].rearrange("p b s -> p (b s)"), t32[:, k % 2, :],
                               p_hi[:, k % PRING].rearrange("p b s -> p (b s)")).then_inc(lo_ready.sem, 1)
                    elif s == ("pv", KV - 2, 2):
                        for t in range(EARLY):
                            pool.wait_ge(o_hi_done.sem, o_hi_done.at(i, t + 1))
                            lo(o_part(False, t), o32[:, t, :], o_part(True, t)).then_inc(oe_ready.sem, 1)
                    elif kind == "gate":
                        b, v = fill(i, ("ln2T", KC - 1))
                        pool.wait_ge(full[b], v)
                        waited(pool)
                        nc.gpsimd.memset(gate_ones[:, :], 1.0).then_inc(ones_ready.sem, 1)
                    elif kind in ("exp", "up"):
                        n = t32_order(s)
                        pool.wait_ge(t_hi_done.sem, t_hi_done.at(i, n + 1))
                        hi, dst = (moe_hi, moe_lo) if kind == "exp" else (h_hi, h_lo)
                        lo(dst[:, s[1], :], t32[:, n % 2, :], hi[:, s[1], :]).then_inc(lo_ready.sem, 1)

                    for v in SPLITS.get(s, ()):
                        if may_split(v, last):
                            split_w(i, v)
                    if kind == "kv" and s[1] == 0 and s[2] + 2 < KC:
                        split_c(i, s[2] + 2)
                    if kind == "down" and s[1] == 1 and s[2] >= DC - 2 and not last:
                        split_c(i + 1, s[2] - (DC - 2))

            over_blocks(pool, body)

        @block.vector
        def _(dve):
            v_ = nc.vector
            links = [0]

            def link(i, op):
                links[0] += 1
                op.then_inc(dve_chain.sem, 1)
                dve.wait_ge(dve_chain.sem, AHEAD_LINKS + dve_chain.at(i, links[0]) if i is not None else links[0])

            def when_full(i, job):
                b, v = fill(i, job)
                dve.wait_ge(full[b], v)
                return b

            def stats(src, tt, h):
                return v_.bn_stats(bn[:, tt, h, :], src[:, tt, h * HALF:(h + 1) * HALF])

            def variance(i, tiles):
                waited(dve)
                for tt in tiles:
                    op = v_.bn_aggr(mv[:, tt, :], bn[:, tt, :, :].rearrange("p a b -> p (a b)"))
                link(i, op)
                t = slice(tiles[0], tiles[-1] + 1)
                v_.tensor_scalar(var[:, t], mv[:, t, 1], EPS, None, ALU.add).then_inc(var_ready.sem, 1)

            def refine(i, ki, k, tiles):
                t = slice(tiles[0], tiles[-1] + 1)
                dve.wait_ge(rstd_guess.sem, rstd_guess.at(ki, k))
                link(i, v_.tensor_tensor(newt[:, t], rstd0[:, t], rstd0[:, t], ALU.mult))
                link(i, v_.scalar_tensor_tensor(newt[:, t], newt[:, t], -0.5, var[:, t], ALU.mult, ALU.mult))
                link(i, v_.scalar_tensor_tensor(rstd[:, t], newt[:, t], 1.5, rstd0[:, t], ALU.add, ALU.mult))

            def mean_var(i, ki, k):
                variance(i, range(TT))
                refine(i, ki, k, range(TT))

            def layernorm(dst, src, tt):
                return v_.tensor_scalar(dst[:, tt, :], src[:, tt, :], mv[:, tt, 0:1], rstd[:, tt:tt + 1],
                                        ALU.subtract, ALU.mult)

            def lo(out_, x32, hi):
                return v_.tensor_tensor(out_, x32, hi.bitcast(F32), ALU.subtract)

            def finish(i, tt):
                link(i, v_.scalar_tensor_tensor(y[:, tt, :], y[:, tt, :], mv[:, tt, 0:1], gam[:, :],
                                                ALU.subtract, ALU.mult))
                v_.scalar_tensor_tensor(y[:, tt, :], y[:, tt, :], rstd[:, tt:tt + 1], x2[:, tt, :],
                                        ALU.mult, ALU.add).then_inc(y_ready.sem, 1)

            link(None, v_.memset(row_max[:, :], 0.0))
            dve.wait_ge(ident_ready, 1)
            link(None, v_.tensor_scalar(neg_mask[:, :], ident[0:GROUP, 0:GROUP], -1.0, None, ALU.mult))
            for tt in range(TT):
                dve.wait_ge(x_loaded[tt].sem, 16)
                stats(rows, tt, 0)
                op = stats(rows, tt, 1)
                if tt % 2:
                    link(None, op)
                    variance(None, [tt - 1, tt])
                    refine(None, 0, tt // 2 - 1, [tt - 1, tt])
                    for t in (tt - 1, tt):
                        layernorm(rows, rows, t).then_inc(xn_ready.sem, 1)
            for kc in range(KC):
                b = when_full("ahead", ("ln1T", kc))
                dve.wait_ge(x1_hi.sem, kc + 1)
                lo(x_lo[:, kc, :], bank[b][:, :], x_hi[:, kc, :]).then_inc(read[b], 1)
            dve.wait_ge(tanh_ready, 1)
            assert links[0] == AHEAD_LINKS, links[0]

            def body(i, last):
                links[0] = 0
                for s in VECTOR_STEPS:
                    kind = s[0]
                    if kind == "kv" and s[2] == KC - 1:
                        src = s[1]
                        if src == 0:
                            when_full(i, ("kv", 0, 0))
                            v_.memset(k_hi[96:96 + GROUP].rearrange("p g b c s -> p (g b c s)").bitcast(F32), 1.0)
                        for t in range(HT):
                            b = when_full(i, ("kv", src, t))
                            dve.wait_ge(kv_hi.sem, kv_hi.at(i, src * (HT + TT) + t + 1))
                            lo(k_lo[0:96, t, :, src, :], bank[b][0:96, :].rearrange("p (b s) -> p b s", b=BPB),
                               k_hi[0:96, t, :, src, :])
                            lo(k_lo[32 * t:32 * t + 32, 3, :, src, :],
                               bank[b][96:128, :].rearrange("p (b s) -> p b s", b=BPB),
                               k_hi[32 * t:32 * t + 32, 3, :, src, :]).then_inc(read[b], 1)
                        for tt in range(TT):
                            b = when_full(i, ("kv", src, HT + tt))
                            dve.wait_ge(kv_hi.sem, kv_hi.at(i, src * (HT + TT) + HT + tt + 1))
                            lo(v_lo[:, src, tt, :, :], bank[b][:, 0:KV * HD].rearrange("p (g d) -> p g d", g=KV),
                               v_hi[:, src, tt, :, 0:HD]).then_inc(read[b], 1)
                    elif kind == "q":
                        g, t = s[1:]
                        b = when_full(i, s)
                        dve.wait_ge(q_hi_done.sem, q_hi_done.at(i, g * HT + t + 1))
                        lo(q_lo[g % 2][0:96, t, :], bank[b][0:96, :], q_hi[g % 2][0:96, t, :])
                        lo(q_lo[g % 2][32 * t:32 * t + 32, 3, :], bank[b][96:128, :],
                           q_hi[g % 2][32 * t:32 * t + 32, 3, :]).then_inc(read[b], 1)
                    elif kind == "max":
                        g, h = s[1:]
                        if h == 0 and g:
                            b, v = fill(i, ("maxT", g - 1))
                            dve.wait_ge(full[b], v)
                        for tt in range(TT):
                            b = when_full(i, s + (tt,))
                            v_.reduce_max(row_max[:, tt * GROUP + h:tt * GROUP + h + 1], bank[b][:, :],
                                          AX.X).then_inc(read[b], 1)
                    elif kind == "maxT":
                        g = s[1]
                        b = when_full(i, s)
                        v_.tensor_tensor(q_hi[g % 2][96:96 + GROUP, :, :],
                                         bank[b][0:GROUP, :].unsqueeze(1).broadcast_to([GROUP, GROUP, TOK]),
                                         neg_mask[:, :].unsqueeze(2).broadcast_to([GROUP, GROUP, TOK]),
                                         ALU.mult).then_inc(read[b], 1)
                    elif kind == "pv":
                        g, n = s[1:]
                        bt, pair = n // 2, n % 2
                        b = when_full(i, s)
                        acc = bank[b][:, :].rearrange("p (h s) -> p h s", h=2)
                        dve.wait_ge(inv_ready.sem, inv_ready.at(i, g * 4 + n + 1))
                        r = slice(32 * (n % 2), 32 * (n % 2) + 32)
                        guess, inv = inv_guess[r], neg_inv[r]
                        link(i, v_.tensor_tensor(inv, acc[96:128], guess, ALU.mult))
                        link(i, v_.scalar_tensor_tensor(inv, inv, 2.0, guess, ALU.subtract, ALU.mult))
                        o_t = o32[:, HT * g:HT * g + HT, :].rearrange("p t (b s) -> p t b s", b=BPB)
                        for j in range(HT):
                            r = slice(32 * j, 32 * j + 32)
                            if pair == 0:
                                op = v_.scalar_tensor_tensor(o_t[r, 0:2, bt, :], acc[r], -1.0, inv,
                                                             ALU.mult, ALU.mult)
                            else:
                                v_.scalar_tensor_tensor(o_t[r, 2, bt, :], acc[r, 0, :], -1.0, inv[:, 0, :],
                                                        ALU.mult, ALU.mult)
                                op = v_.scalar_tensor_tensor(o_t[96:128, j, bt, :], acc[r, 1, :], -1.0,
                                                             inv[:, 1, :], ALU.mult, ALU.mult)
                        op.then_inc(read[b], 1)
                    elif kind == "score":
                        for kt in range(4):
                            k = s[1] * 16 + s[2] * 4 + kt
                            if k in LO_DVE:
                                b, v = fill(i, s + (kt,))
                                dve.wait_ge(read[b], v + 1)
                                lo(p_lo[:, k % PRING].rearrange("p b s -> p (b s)"), t32[:, k % 2, :],
                                   p_hi[:, k % PRING].rearrange("p b s -> p (b s)")).then_inc(lo_ready_dve.sem, 1)
                    elif kind == "o" and s[1] == 0 and s[2] < OT // 2 - 1:
                        for t in late_tiles(s[2]):
                            dve.wait_ge(o_hi_done.sem, o_hi_done.at(i, t + 1))
                            lo(o_part(False, t), o32[:, t, :], o_part(True, t)).then_inc(o_ready.sem, 1)
                    elif kind == "o" and s[2] == OT // 2 - 1:
                        half = s[1]
                        for tt in range(TT):
                            b = when_full(i, ("o", half, tt))
                            xs = x2[:, tt, half * HALF:(half + 1) * HALF]
                            if half == 0:
                                dve.wait_ge(xres_loaded[tt].sem, xres_loaded[tt].at(i, 1))
                            op = v_.scalar_tensor_tensor(xs, bank[b][:, :], tg[:, 0:1], xs, ALU.mult, ALU.add)
                            op.then_inc(read[b], 1)
                            b, v = fill(i, ("o", half, tt))
                            dve.wait_ge(read[b], v + 1)
                            op = stats(x2, tt, half)
                            if half == 1 and tt % 2:
                                link(i, op)
                                variance(i, [tt - 1, tt])
                                refine(i, i, 1 + tt // 2, [tt - 1, tt])
                                t = slice(tt - 1, tt + 1)
                                v_.scalar_tensor_tensor(nmr[:, t], mv[:, t, 0], -1.0, rstd[:, t], ALU.mult,
                                                        ALU.mult).then_inc(ln2_scales.sem, 1)
                        if half == 1:
                            layernorm(rows, x2, TT - 1).then_inc(xn2_last.sem, 1)
                    elif kind == "o" and U_LO_DVE in SPLITS[s]:
                        k = U_LO_DVE % 2
                        dve.wait_ge(w_hi_done.sem, w_hi_done.at(i, U_LO_DVE + 1))
                        lo(w_lo[:, k, :], w_st[:, k, :], w_hi[:, k, :]).then_inc(w_ready_dve.sem, 1)
                    elif kind == "ln2T":
                        b = when_full(i, s)
                        dve.wait_ge(x2_hi.sem, x2_hi.at(i, s[1] + 1))
                        lo(x_lo[:, s[1], :], bank[b][:, :], x_hi[:, s[1], :]).then_inc(read[b], 1)
                    elif kind == "gateT":
                        b = when_full(i, s)
                        t4 = bank[b][:, :].rearrange("p (t e) -> p t e", t=TT)
                        link(i, v_.tensor_copy(logits[:, :, :], t4[:, :, 0:EXPERTS]))
                        v_.tensor_tensor(logits[:, :, :], logits[:, :, :], t4[:, :, 32:32 + EXPERTS],
                                         ALU.add).then_inc(read[b], 1)
                        b, v = fill(i, s)
                        dve.wait_ge(read[b], v + 1)
                        waited(dve)
                        for tt in range(TT):
                            op = v_.max(top8[:, tt, :], logits[:, tt, :])
                        link(i, op)
                        link(i, v_.tensor_tensor(r_sum[:, :], top8[:, :, 0], top8[:, :, 1], ALU.add))
                        for tt in range(TT):
                            op = v_.tensor_scalar(r_diag[:, tt * P:(tt + 1) * P], ident[:, :], r_sum[:, tt:tt + 1],
                                                  None, ALU.mult)
                        op.then_inc(diag_ready.sem, 1)
                    elif kind == "fc1":
                        b = when_full(i, s)
                        dve.wait_ge(lat_hi_done.sem, lat_hi_done.at(i, s[1] + 1))
                        lo(lat_lo[:, s[1], :], bank[b][:, :], lat_hi[:, s[1], :]).then_inc(read[b], 1)
                    elif kind == "exp":
                        n = t32_order(s)
                        b, v = fill(i, ("rbc",))
                        dve.wait_ge(read[b], v + 1)
                        b = when_full(i, s)
                        lo_done(dve, i, KV * 16 + n - 2)
                        v_.tensor_tensor(t32[:, n % 2, :], bank[b][:, :], r_bc[:, :], ALU.mult).then_inc(read[b], 1)
                    elif kind == "up":
                        n = t32_order(s)
                        b = when_full(i, s)
                        dve.wait_ge(relu_done.sem, relu_done.at(i, s[1] + 1))
                        v_.scalar_tensor_tensor(t32[:, n % 2, :], bank[b][:, :], 0.0, t32[:, n % 2, :],
                                                ALU.max, ALU.mult).then_inc(read[b], 1)
                    elif kind == "down" and s[1:] == (0, 0) and not last:
                        for tt in range(TT):
                            dve.wait_ge(x_loaded[tt].sem, x_loaded[tt].at(i + 1, 1))
                            stats(rows, tt, 0)
                            op = stats(rows, tt, 1)
                        link(i, op)
                        mean_var(i, i, 3)
                        for tt in range(TT):
                            layernorm(rows, rows, tt).then_inc(xn_ready.sem, 1)
                    elif kind == "ln1T" and not last:
                        b = when_full(i, s)
                        dve.wait_ge(x1_hi.sem, x1_hi.at(i + 1, s[1] + 1))
                        lo(x_lo[:, s[1], :], bank[b][:, :], x_hi[:, s[1], :]).then_inc(read[b], 1)
                    elif kind == "down" and s[2] == DC - 1:
                        for tt in range(TT):
                            b, v = fill(i, ("down", s[1], tt))
                            dve.wait_ge(read[b], v + 1)
                            op = stats(y, tt, s[1])
                            if s[1] == 1 and last:
                                link(i, op)
                                variance(i, [tt])
                                for t in range(max(tt - 1, 0), tt + (tt == TT - 1)):
                                    refine(i, i, 3 + t, [t])
                                    finish(i, t)
                        if s[1] == 1 and not last:
                            link(i, op)
                            mean_var(i, i, 4)
                            for tt in range(TT):
                                finish(i, tt)
                    if kind == "down" and s[1:] == (0, 2):
                        dve.wait_ge(gb_loaded.sem, gb_loaded.at(i, 2))
                        v_.tensor_scalar(bet[:, :], bet[:, :], tg[:, 1:2], None, ALU.mult)
                        link(i, v_.tensor_scalar(gam[:, :], gam[:, :], tg[:, 1:2], None, ALU.mult))
                    elif kind == "down" and s[1] == 0 and 3 <= s[2] < 3 + TT:
                        tt = s[2] - 3
                        op = v_.tensor_tensor(x2[:, tt, :], x2[:, tt, :], bet[:, :], ALU.add)
                        if tt == TT - 1:
                            link(i, op)
                assert last or links[0] == DVE_LINKS, links[0]

            over_blocks(dve, body)

        @block.tensor
        def _(pe):
            mm = nc.tensor.matmul

            def split_product(out_, w, wl, m, ml, first, final):
                mm(out_, w, m, start=first, stop=False)
                mm(out_, w, ml, start=False, stop=False)
                return mm(out_, wl, m, start=False, stop=final)

            def when_free(i, job):
                b, v = fill(i, job)
                pe.wait_ge(read[b], v)
                return b

            def when_read(i, job):
                b, v = fill(i, job)
                pe.wait_ge(read[b], v + 1)

            def maximum_tile(i, job):
                g, h, tt = job[1:]
                if tt == 0:
                    pe.wait_ge(q_hi_done.sem, q_hi_done.at(i, g * HT + min(h, HT - 1) + 1))
                if job[1:] == (0, 0, 0):
                    pe.wait_ge(kv_hi.sem, kv_hi.at(i, (HT + TT) + HT))
                b = when_free(i, job)
                mm(bank[b][:, :], q_hi[g % 2][0:HD, h, tt * P:(tt + 1) * P],
                   k_hi[0:HD, g, tt // 2, :, :].rearrange("p c s -> p (c s)"),
                   start=True, stop=True).then_inc(full[b], 1)

            def transpose_maxima(i, job):
                when_read(i, ("max", job[1], GROUP - 1, TT - 1))
                b = when_free(i, job)
                for tt in range(TT):
                    op = nc.tensor.transpose(bank[b][:, tt * P:(tt + 1) * P],
                                             row_max[:, tt * GROUP:tt * GROUP + P], ident[:, :])
                op.then_inc(full[b], 1)

            def ride(i, s, at):
                for job, k in RIDERS.get(s, ()):
                    if k == at:
                        (maximum_tile if job[0] == "max" else transpose_maxima)(i, job)

            def transpose_tile(i, job, tt):
                kc = job[1]
                b = when_free(i, job) if tt == 0 else fill(i, job)[0]
                op = nc.tensor.transpose(bank[b][:, tt * P:(tt + 1) * P], rows[:, tt, kc * P:(kc + 1) * P],
                                         ident[:, :])
                if tt == TT - 1:
                    op.then_inc(full[b], 1)

            def transpose_rows(i, job, kc):
                b = when_free(i, job)
                for tt in range(TT):
                    op = nc.tensor.transpose(bank[b][:, tt * P:(tt + 1) * P], rows[:, tt, kc * P:(kc + 1) * P],
                                             ident[:, :])
                op.then_inc(full[b], 1)

            pe.wait_ge(ident_ready, 1)
            for tt in range(TT):
                pe.wait_ge(xn_ready.sem, tt + 1)
                for kc in range(KC):
                    transpose_tile("ahead", ("ln1T", kc), tt)
            pe.wait_ge(gate_ready, 1)

            def body(i, last):
                for s in STEPS:
                    kind, u = s[0], unit_of(s)
                    if kind == "exp":
                        u = U_EXP + s[1] // 2
                    units = {"o": OT // 2, "down": DC}.get(kind)
                    joined = units and s[1] == 1 and s[2] >= units - 2 and (kind == "o" or last)
                    if joined and s[2] == units - 2 or s == ("fc1", 0):
                        continue
                    if kind == "gate":
                        u = U_FC1
                    if u is not None:
                        if not joined:
                            unit_split(pe, i, u)
                        wh, wl = w_hi[:, u % 2, :], w_lo[:, u % 2, :]
                    op = None
                    if kind == "kv":
                        src, kc = s[1:]
                        if src == 0:
                            pe.wait_ge(c_ready.sem, c_ready.at(i, kc + 1))
                            ah, al = c_hi[:, kc % 2, :], c_lo[:, kc % 2, :]
                        else:
                            ah, al = x_hi[:, kc, :], x_lo[:, kc, :]
                            if kc == 0:
                                b, _ = BANK[("ln1T", KC - 1)]
                                pe.wait_ge(read[b], i * FILLS[b] + (FILLS_AHEAD[b] + 1))
                        first, final = kc == 0, kc == KC - 1
                        for t in range(HT):
                            job = ("kv", src, t)
                            b = when_free(i, job) if first else fill(i, job)[0]
                            op = split_product(bank[b][:, :], wh[:, t * P:(t + 1) * P], wl[:, t * P:(t + 1) * P],
                                               ah, al, first, final)
                            if final:
                                op.then_inc(full[b], 1)
                        for tt in range(TT):
                            job = ("kv", src, HT + tt)
                            b = when_free(i, job) if first else fill(i, job)[0]
                            tok = slice(tt * P, (tt + 1) * P)
                            op = split_product(bank[b][:, 0:KV * HD], ah[:, tok], al[:, tok],
                                               wh[:, HT * P:KVW], wl[:, HT * P:KVW], first, final)
                            if final:
                                op.then_inc(full[b], 1)
                    elif kind in ("q", "fc1", "up"):
                        b = when_free(i, s)
                        for kc in range(KC):
                            c = slice(kc * P, (kc + 1) * P)
                            op = split_product(bank[b][:, :], wh[:, c], wl[:, c], x_hi[:, kc, :], x_lo[:, kc, :],
                                               kc == 0, kc == KC - 1)
                            if kc == KC - 1:
                                op.then_inc(full[b], 1)
                            ride(i, s, kc)
                    elif kind == "exp":
                        if s[1] == 0:
                            when_read(i, ("fc1", LT - 1))
                        b = when_free(i, s)
                        for kc in range(LT):
                            at = ((s[1] % 2) * LT + kc) * P
                            op = split_product(bank[b][:, :], wh[:, at:at + P], wl[:, at:at + P],
                                               lat_hi[:, kc, :], lat_lo[:, kc, :], kc == 0, kc == LT - 1)
                        op.then_inc(full[b], 1)
                    elif kind == "maxT" and s[1]:
                        transpose_maxima(i, s)
                    elif kind == "score":
                        g, n = s[1:]
                        bt, pair = n // 2, n % 2
                        if n == 0:
                            pe.wait_ge(ones_ready.sem, ones_ready.at(i, 1))
                            when_read(i, ("maxT", g))
                        heads, tok = slice(2 * pair, 2 * pair + 2), slice(bt * SEQ, (bt + 1) * SEQ)
                        A = HD + GROUP
                        for kt in range(4):
                            b = when_free(i, s + (kt,))
                            keys = slice(kt % 2 * P, (kt % 2 + 1) * P)
                            mm(bank[b][:, :], k_hi[0:A, g, bt, kt // 2, keys], q_hi[g % 2][0:A, heads, tok],
                               start=True, stop=False)
                            mm(bank[b][:, :], k_hi[0:HD, g, bt, kt // 2, keys], q_lo[g % 2][0:HD, heads, tok],
                               start=False, stop=False)
                            mm(bank[b][:, :], k_lo[0:HD, g, bt, kt // 2, keys], q_hi[g % 2][0:HD, heads, tok],
                               start=False, stop=True).then_inc(full[b], 1)
                            ride(i, s, kt)
                    elif kind == "pv":
                        g, n = s[1:]
                        b = when_free(i, s)
                        for kt in range(4):
                            k = g * 16 + n * 4 + kt
                            lo_done(pe, i, k)
                            tt = n // 2 * 2 + kt % 2
                            ph, pl = (p[:, k % PRING].rearrange("p b s -> p (b s)") for p in (p_hi, p_lo))
                            mm(bank[b][:, :], v_hi[:, kt // 2, tt, g, :], ph, start=kt == 0, stop=False)
                            mm(bank[b][0:HD, :], v_lo[:, kt // 2, tt, g, :], ph, start=False, stop=False)
                            op = mm(bank[b][:, :], v_hi[:, kt // 2, tt, g, :], pl, start=False, stop=kt == 3)
                            if kt < 3:
                                op.then_inc(p_used.sem, 1)
                        op.then_inc(full[b], 1)
                    elif kind in ("o", "down"):
                        half, c = s[1:]
                        n_chunks = 2 * units
                        parts = []
                        for t in range(2 * (c - joined), 2 * c + 2):
                            v = u - c + t // 2
                            w = slice(t % 2 * HALF, (t % 2 + 1) * HALF)
                            wh, wl = w_hi[:, v % 2, w], w_lo[:, v % 2, w]
                            if kind == "o":
                                parts.append((t, o_part(True, t), o_part(False, t), wh, wl))
                            elif t < LT:
                                parts.append((t, moe_hi[:, t, :], moe_lo[:, t, :], wh, wl))
                            else:
                                parts.append((t, h_hi[:, t - LT, :], h_lo[:, t - LT, :], wh, wl))
                        if half == 0:
                            if kind == "down":
                                lo_done(pe, i, KV * 16 + t32_order(("exp", t) if t < LT else ("up", t - LT)))
                            elif t < EARLY:
                                pe.wait_ge(oe_ready.sem, oe_ready.at(i, t + 1))
                            else:
                                pe.wait_ge(o_ready.sem, o_ready.at(i, t - EARLY + 1))
                        order = [(tt, parts) for tt in range(TT)]
                        if joined:
                            p0, p1 = parts[:2], parts[2:]
                            order = [(0, p0), (1, p0), (0, p1), (1, p1), (2, parts), (3, parts)]
                        for tt, some in order:
                            job, tok = (kind, half, tt), slice(tt * P, (tt + 1) * P)
                            b = when_free(i, job) if c == 0 else fill(i, job)[0]
                            if joined and tt == 0:
                                unit_split(pe, i, u - (some is p0))
                            for t, ah, al, wh, wl in some:
                                op = split_product(bank[b][:, :], ah[:, tok], al[:, tok], wh, wl,
                                                   t == 0, t == n_chunks - 1)
                                if t == n_chunks - 3 and joined and tt == TT - 1:
                                    op.then_inc(w_used.sem, 1)
                            if t == n_chunks - 1:
                                op.then_inc(full[b], 1)
                    elif kind == "ln2T":
                        for tt in range(TT if s[1] == 0 else 0):
                            if tt < TT - 1:
                                pe.wait_ge(xn2_ready.sem, xn2_ready.at(i, tt + 1))
                            else:
                                pe.wait_ge(xn2_last.sem, xn2_last.at(i, 1))
                            for kc in range(KC):
                                transpose_tile(i, ("ln2T", kc), tt)
                    elif kind == "ln1T" and not last:
                        if s[1] == 0:
                            pe.wait_ge(xn_ready.sem, xn_ready.at(i + 1, TT))
                        transpose_rows(i, s, s[1])
                    elif kind == "gate":
                        f = ("fc1", 0)
                        bg, bf = fill(i, s)[0], fill(i, f)[0]
                        for kc in range(KC):
                            c, g_w = slice(kc * P, (kc + 1) * P), gate_w[:, kc, :]
                            first, final = kc == 0, kc == KC - 1
                            pe.wait_ge(x2_hi.sem, x2_hi.at(i, kc + 1))
                            if first:
                                when_free(i, s)
                            mm(bank[bg][0:GPAD, :], g_w, x_hi[:, kc, :], start=first, stop=False)
                            if first:
                                when_free(i, f)
                            mm(bank[bf][:, :], wh[:, c], x_hi[:, kc, :], start=first, stop=False)
                            mm(bank[bf][:, :], wl[:, c], x_hi[:, kc, :], start=False, stop=False)
                            when_read(i, ("ln2T", kc))
                            op = mm(bank[bg][0:GPAD, :], g_w, x_lo[:, kc, :], start=False, stop=final)
                            if final:
                                op.then_inc(full[bg], 1)
                            op = mm(bank[bf][:, :], wh[:, c], x_lo[:, kc, :], start=False, stop=final)
                        op.then_inc(full[bf], 1)
                    elif kind == "gateT":
                        when_read(i, ("gate",))
                        b = when_free(i, s)
                        for tt in range(TT):
                            op = nc.tensor.transpose(bank[b][:, tt * P:tt * P + GPAD],
                                                     gate_log[0:GPAD, tt * P:(tt + 1) * P], ident[0:GPAD, 0:GPAD])
                        op.then_inc(full[b], 1)
                    elif kind == "rbc":
                        pe.wait_ge(ones_ready.sem, ones_ready.at(i, 2))
                        pe.wait_ge(diag_ready.sem, diag_ready.at(i, 1))
                        b = when_free(i, s)
                        mm(bank[b][:, :], gate_ones[:, :], r_diag[:, :], start=True, stop=True).then_inc(full[b], 1)
                    if u in COUNTED:
                        op.then_inc(w_used.sem, 1)

            over_blocks(pe, body)


def kernel(x, ctx_4096, g_xattn, g_ffn, L0_xattn_Wq, L0_xattn_Wk, L0_xattn_Wv, L0_xattn_Wo, L0_ffn_gate_w,
           L0_ffn_up_w, L0_ffn_down_w, L0_ffn_fc1_w, L0_ffn_fc2_w, L0_ffn_expert_w, L0_ffn_ln_gamma, L0_ffn_ln_beta):
    import numpy as np
    import concourse.bacc as bacc
    from concourse.bass_utils import run_bass_kernel_spmd

    x, ctx, Wq, Wk, Wv, Wo, gate, up, down, fc1, fc2, expert, gamma, beta = (np.asarray(a) for a in (
        x, ctx_4096, L0_xattn_Wq, L0_xattn_Wk, L0_xattn_Wv, L0_xattn_Wo, L0_ffn_gate_w, L0_ffn_up_w, L0_ffn_down_w,
        L0_ffn_fc1_w, L0_ffn_fc2_w, L0_ffn_expert_w, L0_ffn_ln_gamma, L0_ffn_ln_beta))
    group = np.concatenate([np.r_[t * HD:(t + 1) * HD, 3 * HD + 32 * t:3 * HD + 32 * t + 32] for t in range(HT)])
    order = np.concatenate([g * GROUP * HD + group for g in range(KV)])

    def stationary(w, chunks, tiles=1):
        n = w.shape[1] // (P * tiles)
        return w.reshape(chunks, P, n, tiles, P).transpose(2, 1, 3, 0, 4).reshape(n, P, tiles * chunks * P)

    def moving(w):
        n = w.shape[0] // (2 * P)
        return w.reshape(n, 2, P, 2, HALF).transpose(3, 0, 2, 1, 4).reshape(2 * n, P, DIM)

    arrays = {
        "x": x.reshape(-1, DIM),
        "ctxT": ctx.reshape(BLOCKS, TOK, KC, P).transpose(0, 2, 3, 1),
        "g_x": g_xattn, "g_f": g_ffn,
        "w_kv": np.concatenate([Wk.T[:, group], Wv.T], axis=1).reshape(KC, P, KVW),
        "w_q": stationary(Wq.T[:, order], KC),
        "w_o": moving(Wo.T[order]),
        "w_fc1": stationary(fc1, KC),
        "w_exp": stationary(expert, LT, 2),
        "w_up": stationary(up, KC),
        "w_down": moving(np.concatenate([fc2, down])),
        "w_gate": gate.reshape(KC, P, EXPERTS).transpose(1, 0, 2),
        "gamma": gamma, "beta": beta,
    }
    arrays = {f"in_{k}": np.ascontiguousarray(np.asarray(a)) for k, a in arrays.items()}
    nc = bacc.Bacc("TRN2", target_bir_lowering=False, num_devices=1)
    args = [nc.dram_tensor(k, a.shape, F32, kind="ExternalInput").ap() for k, a in arrays.items()]
    args.append(nc.dram_tensor("out", (BATCH * SEQ, DIM), F32, kind="ExternalOutput").ap())
    layer_kernel(nc, *args)
    r = run_bass_kernel_spmd(nc, [arrays], core_ids=[0])
    return r.results[0]["out"].reshape(BATCH, SEQ, DIM)
```
